# Optimizing a Trainium2 kernel written in Bass

```python
import numpy as np
import jax
import jax.numpy as jnp

def _softmax(x, axis=-1):
    return jax.nn.softmax(x, axis=axis)

def _gelu(x):
    return jax.nn.gelu(x, approximate=True)

def _silu(x):
    return jax.nn.silu(x)

def _sigmoid(x):
    return jax.nn.sigmoid(x)

def _layernorm(x, axis=-1, eps=1e-05):
    m = jnp.mean(x, axis=axis, keepdims=True)
    v = jnp.var(x, axis=axis, keepdims=True)
    return (x - m) / jnp.sqrt(v + eps)

def _scatter_add(tgt, idx, src, axis=0):
    return tgt.at[idx].add(src)

def _segment_sum(src, seg, n):
    return jax.ops.segment_sum(src, seg, n)
kernel_name = 'mk_seq_preln_d1_jaxref_r4_98ef9d'

def setup_inputs(seed: int=0):
    np.random.seed(seed)
    _w = jnp.asarray

    def _L0_attn_setup():
        import jax, jax.numpy as jnp
        import numpy as np
        D_MODEL = 256
        NUM_HEADS = 16
        key = jax.random.key(seed)
        ks = jax.random.split(key, 5)
        x = jax.random.normal(ks[0], (1, 1024, D_MODEL), dtype=jnp.float32)
        scale = 0.02
        wq = jax.random.normal(ks[1], (D_MODEL, D_MODEL), dtype=jnp.float32) * scale
        wk = jax.random.normal(ks[2], (D_MODEL, D_MODEL), dtype=jnp.float32) * scale
        wv = jax.random.normal(ks[3], (D_MODEL, D_MODEL), dtype=jnp.float32) * scale
        wo = jax.random.normal(ks[4], (D_MODEL, D_MODEL), dtype=jnp.float32) * scale
        return {'x': x, 'wq': wq, 'wk': wk, 'wv': wv, 'wo': wo}
    _L0_attn_in = _L0_attn_setup()

    def _L0_ffn_setup():
        import jax, jax.numpy as jnp
        import numpy as np
        DIM = 256

        def _reference_tuple_inner(x, W_r, W_k, W_v, mu_r, mu_k):
            B, T, C = x.shape
            x_prev = jnp.concatenate([jnp.zeros((B, 1, C), x.dtype), x[:, :-1, :]], axis=1)
            xr = mu_r * x + (1.0 - mu_r) * x_prev
            xk = mu_k * x + (1.0 - mu_k) * x_prev
            r = jax.nn.sigmoid(jnp.einsum('btc,dc->btd', xr, W_r))
            k = jnp.einsum('btc,dc->btd', xk, W_k)
            k_act = jnp.square(jax.nn.relu(k))
            out = r * jnp.einsum('btc,dc->btd', k_act, W_v)
            new_state = x[:, -1, :]
            return (out, new_state)
        key = jax.random.key(seed)
        ks = jax.random.split(key, 6)
        B, T, C = (8, 512, DIM)
        x = jax.random.normal(ks[0], (B, T, C), dtype=jnp.float32)
        s = 1.0 / np.sqrt(C)
        W_r = jax.random.uniform(ks[1], (C, C), jnp.float32, -s, s)
        W_k = jax.random.uniform(ks[2], (C, C), jnp.float32, -s, s)
        W_v = jax.random.uniform(ks[3], (C, C), jnp.float32, -s, s)
        mu_r = jax.random.uniform(ks[4], (C,), jnp.float32)
        mu_k = jax.random.uniform(ks[5], (C,), jnp.float32)
        return {'x': x, 'W_r': W_r, 'W_k': W_k, 'W_v': W_v, 'mu_r': mu_r, 'mu_k': mu_k}
    _L0_ffn_in = _L0_ffn_setup()
    _d = {'L0_attn_x': _L0_attn_in['x'], 'L0_attn_wq': _L0_attn_in['wq'], 'L0_attn_wk': _L0_attn_in['wk'], 'L0_attn_wv': _L0_attn_in['wv'], 'L0_attn_wo': _L0_attn_in['wo'], 'L0_ffn_W_r': _L0_ffn_in['W_r'], 'L0_ffn_W_k': _L0_ffn_in['W_k'], 'L0_ffn_W_v': _L0_ffn_in['W_v'], 'L0_ffn_mu_r': _L0_ffn_in['mu_r'], 'L0_ffn_mu_k': _L0_ffn_in['mu_k']}
    _x0 = _d['L0_attn_x']
    _d['L0_attn_x'] = jax.random.normal(jax.random.fold_in(jax.random.key(seed), 1), (1, 4096, 256), dtype=_x0.dtype)
    del _x0
    return _d

def reference(L0_attn_x, L0_attn_wq, L0_attn_wk, L0_attn_wv, L0_attn_wo, L0_ffn_W_r, L0_ffn_W_k, L0_ffn_W_v, L0_ffn_mu_r, L0_ffn_mu_k):

    def _L0_attn_ref(x, wq, wk, wv, wo):
        import jax, jax.numpy as jnp
        import numpy as np
        D_MODEL = 256
        NUM_HEADS = 16
        B, S, D = x.shape
        H = NUM_HEADS
        d_k = D // H
        q = x @ wq.T
        k = x @ wk.T
        v = x @ wv.T
        qh = q.reshape(B, S, H, d_k).transpose(0, 2, 1, 3)
        kh = k.reshape(B, S, H, d_k).transpose(0, 2, 1, 3)
        vh = v.reshape(B, S, H, d_k).transpose(0, 2, 1, 3)
        scores = jnp.einsum('bhqd,bhkd->bhqk', qh, kh) / jnp.sqrt(jnp.asarray(d_k, x.dtype))
        causal = jnp.tril(jnp.ones((S, S), dtype=bool))
        scores = jnp.where(causal, scores, jnp.asarray(-10000.0, x.dtype))
        attn = jax.nn.softmax(scores, axis=-1)
        ctx = jnp.einsum('bhqk,bhkd->bhqd', attn, vh)
        ctx = ctx.transpose(0, 2, 1, 3).reshape(B, S, D)
        return ctx @ wo.T

    def _L0_ffn_ref(x, W_r, W_k, W_v, mu_r, mu_k):
        import jax, jax.numpy as jnp
        import numpy as np
        DIM = 256

        def _reference_tuple_inner(x, W_r, W_k, W_v, mu_r, mu_k):
            B, T, C = x.shape
            x_prev = jnp.concatenate([jnp.zeros((B, 1, C), x.dtype), x[:, :-1, :]], axis=1)
            xr = mu_r * x + (1.0 - mu_r) * x_prev
            xk = mu_k * x + (1.0 - mu_k) * x_prev
            r = jax.nn.sigmoid(jnp.einsum('btc,dc->btd', xr, W_r))
            k = jnp.einsum('btc,dc->btd', xk, W_k)
            k_act = jnp.square(jax.nn.relu(k))
            out = r * jnp.einsum('btc,dc->btd', k_act, W_v)
            new_state = x[:, -1, :]
            return (out, new_state)
        return _reference_tuple_inner(x, W_r, W_k, W_v, mu_r, mu_k)[0]
    x = L0_attn_x
    x = x + _L0_attn_ref(_layernorm(x, axis=-1), L0_attn_wq, L0_attn_wk, L0_attn_wv, L0_attn_wo)
    x = x + _L0_ffn_ref(_layernorm(x, axis=-1), L0_ffn_W_r, L0_ffn_W_k, L0_ffn_W_v, L0_ffn_mu_r, L0_ffn_mu_k)
    return x

_drawn_inputs = setup_inputs


def setup_inputs(seed=0):
    import zlib

    import numpy as np

    out = dict(_drawn_inputs(seed))
    spreads = {}
    factors = {'L0_attn_wq': 8.0,
     'L0_attn_wk': 8.0,
     'L0_attn_wv': 8.0,
     'L0_attn_wo': 8.0,
     'L0_ffn_W_r': 11.889,
     'L0_ffn_mu_r': 35.788,
     'L0_ffn_W_k': 2.727,
     'L0_ffn_mu_k': 4.516}
    for name, (base, spread) in spreads.items():
        noise = np.random.default_rng([zlib.crc32(name.encode()), seed]).standard_normal(out[name].shape)
        drawn = base * np.exp(spread * noise) if base else spread * noise
        out[name] = jnp.asarray(drawn.astype(out[name].dtype))
    for name, factor in factors.items():
        out[name] = (out[name] * factor).astype(out[name].dtype)
    return out
```

```python
from contextlib import ExitStack

import concourse.bass as bass
from concourse import mybir

ALU = mybir.AluOpType
ACT = mybir.ActivationFunctionType
AXX = mybir.AxisListType.X
F32 = mybir.dt.float32
BF16 = mybir.dt.bfloat16
U32 = mybir.dt.uint32

P = 128
S, D, H = 4096, 256, 16
DK = D // H
T = 512
NT = S // T
TB = T // P
NC = D // P
HALF = H // 2
GH = 4
GROUPS = 2 * NT * 2
KSLOTS = NT + 1
QSLOTS = 4
PSLOTS = 8
RING = 3
VW = DK + 1
VP = 152
EPS = 1e-5
NEG = -1e30
GATE_MIN = -87.0
QPARTS = (0, 0, 1, 0, 2, 1)
KPARTS = (0, 1, 0, 2, 0, 1)
BANDS = len(QPARTS)
KR = BANDS * DK
KM = KR + 3


def tile_of(n):
    return n % (2 * NT) // 2


def half_of(n):
    return n // (2 * NT)


def kslot(half, c):
    return (NT * half + c) % KSLOTS


def pace_attention(gap):
    at, start, end, now = [], {}, {}, 0.0
    for n in range(GROUPS):
        now += gap[n]
        start[n] = now
        for kb in range(TB * (tile_of(n) + 1)):
            cols = T - P * max(0, kb - TB * tile_of(n))
            at.append((now, ("keys", n, kb)))
            now += 2.7 * cols / T + 0.2
        end[n] = now
        at.append((now + 2.9, ("ctx_out", n)))
    row_maxima, first_max, due = {}, {}, None
    for n in reversed(range(GROUPS)):
        due = start[n] - 10.0 if due is None else min(due, start[n] - 10.0)
        steps = [(due + 5.0, ("turn_max", n)), (due + 0.01, ("negmax", n))]
        for i in reversed(range(GH)):
            for qt in reversed(range(TB)):
                for p in reversed(range(tile_of(n) + 1)):
                    w = T if p < tile_of(n) else P * (qt + 1)
                    due -= 0.10 + 0.54 * w / T
                    steps.append((due, ("max", n, i, qt, p)))
        row_maxima[n], first_max[n] = steps[::-1], due
    for n in range(GROUPS):
        free = end[n - QSLOTS] + 0.2 if n >= QSLOTS else -1e9
        if n >= 2 * KSLOTS:
            free = max(free, end[2 * NT - 1] + 3.0)
        if n:
            free = max(free, row_maxima[n - 1][-2][0] + 0.01)
        shift = max(0.0, free - first_max[n])
        row_maxima[n] = [(t + shift, step) for t, step in row_maxima[n]]
        first_max[n] += shift
        late = row_maxima[n][-1][0] - start[n]
        if late > 0:
            return n, late, None, None, None
        at += row_maxima[n]
        at.append((max(first_max[n] - 5.0, end[n - QSLOTS] + 0.1 if n >= QSLOTS else -1e9), ("query_load", n)))
    return None, 0.0, at, first_max, end


def make_plan():
    gap = [0.0] * GROUPS
    n, late, at, first_max, end = pace_attention(gap)
    while at is None:
        gap[n] += late + 0.5
        n, late, at, first_max, end = pace_attention(gap)
    for j in range(NT):
        t0 = first_max[2 * j] - 45.0
        if j:
            t0 = max(t0, prev + 1.0)
        at.append((t0, ("x_load", j)))
        at.append((t0 + 4.0, ("ln", j)))
        for c in range(NC):
            at.append((t0 + 8.0 + c, ("turn", j, c)))
        at.append((t0 + 12.0, ("key", j, 0)))
        at.append((t0 + 15.0, ("query", j, 0)))
        at.append((t0 + 21.0, ("key_load", 0, j)))
        at.append((t0 + 22.0, ("value", j, 0)))
        at.append((t0 + 24.0, ("value", j, 1)))
        at.append((t0 + 27.0, ("value_store", j)))
        at.append((t0 + 28.0, ("key", j, 1)))
        at.append((t0 + 31.0, ("query", j, 1)))
        prev = t0 + 31.0
        t1 = first_max[2 * NT + 2 * j] - 12.0
        if j:
            t1 = max(t1, end[2 * NT - 1] + 0.1)
        at.append((t1, ("key_load", 1, j)))
        at.append((t1 + 0.1, ("value_load", j)))
    t = 0.0
    for j in range(NT):
        t = max(t, end[2 * NT + 2 * j + 1] + 5.0)
        at.append((t, ("ctx_load", j)))
        at.append((t, ("x_load", NT + j)))
        at.append((t + 4.0, ("attn_norm", j)))
        at.append((t + 9.0, ("attn_out", j, 0)))
        at.append((t + 10.5, ("attn_out", j, 1)))
        at.append((t + 11.0, ("ln", NT + j)))
        for c in range(NC):
            at.append((t + 16.0 + c, ("turn", NT + j, c)))
        at.append((t + 17.5, ("mix", j)))
        for oc in range(NC):
            at.append((t + 21.0 + 1.5 * oc, ("up", j, oc)))
        for i2 in range(2):
            at.append((t + 24.5 + 1.5 * i2, ("gate", j, i2)))
        for i2 in range(2):
            at.append((t + 28.5 + 1.5 * i2, ("down", j, i2)))
        at.append((t + 32.0, ("out_store", j)))
        t += 33.0
    return [step for _, step in sorted(at, key=lambda a: a[0])]


WORK = ("max", "turn_max", "turn", "key", "query", "value", "attn_out", "up", "gate", "down")


def attention_ffn(nc, x, wq_t, wk_t, wv_t, wo_t, wr_t, wkf_t, wvf_t, mu_r, mu_k, out):
    plan = make_plan()

    number, count, unit_of, units = {}, {}, {}, []
    for step in plan:
        kind = "qk" if step[0] in ("key", "query") else step[0]
        number[step] = count.get(kind, 0)
        count[kind] = number[step] + 1
        if step[0] in WORK:
            unit_of[step] = len(units)
            units.append(step)
    block_of, n_blocks = {}, 0
    for n in range(GROUPS):
        for kb in range(TB * (tile_of(n) + 1)):
            block_of[n, kb] = n_blocks
            n_blocks += 1
    last_block = {n: block_of[n, TB * (tile_of(n) + 1) - 1] for n in range(GROUPS)}
    half0_blocks = last_block[2 * NT - 1] + 1
    max_through = {}
    for step in units:
        if step[0] == "max":
            max_through[step[1]] = number[step] + 1

    def dram(name, shape, dt):
        return nc.dram_tensor(name, shape, dt, kind="Internal").ap()

    q_parts = dram("q_parts", [3, D, S], BF16)
    k_parts = dram("k_parts", [3, D, S], BF16)
    v_other = dram("v_other", [NT, P, TB * VP], F32)
    ctx_dram = dram("ctx_dram", [D, S], F32)
    sum_dram = dram("sum_dram", [H, S], F32)

    with ExitStack() as ctx:
        def sb(name, shape, dt=F32):
            return ctx.enter_context(nc.sbuf_tensor(name, shape, dt))

        def psum(name, shape):
            return ctx.enter_context(nc.psum_tensor(name, shape, F32))

        def sem(name):
            return ctx.enter_context(nc.semaphore(name))

        keys = sb("keys", [P, KSLOTS, HALF, T], BF16)
        queries = sb("queries", [P, QSLOTS, GH, T], BF16)
        values = sb("values", [P, KSLOTS, TB, VP])
        probs = sb("probs", [P, PSLOTS, T])
        w = {name: sb(name, [P, NC, D]) for name in ("wq", "wk", "wv", "wo", "wr", "wkf", "wvf")}
        mu = sb("mu", [P, 2, NC])
        one_minus_mu = sb("one_minus_mu", [P, 2, NC])
        x_in = sb("x_in", [P, 2, TB, D])
        xn = sb("xn", [P, TB, D])
        xnT = sb("xnT", [P, NC, T])
        parts = sb("parts", [P, 2, 3, T], BF16)
        rest = sb("rest", [P, 2, T])
        v_out = sb("v_out", [P, TB, VP])
        bn = sb("bn", [P, TB, 6])
        mean_var = sb("mean_var", [P, TB, 2])
        var_mean = sb("var_mean", [P, 2, TB])
        minus_half = sb("minus_half", [P, TB])
        norm = sb("norm", [P, 2, 2, TB])
        row_max = sb("row_max", [P, 2, GH * TB, NT])
        neg_max = sb("neg_max", [P, 2, GH * TB])
        max_rest = sb("max_rest", [P, GH * TB])
        max_parts = sb("max_parts", [P, 2, 3, GH * TB], BF16)
        max_turned = sb("max_turned", [3 * GH * TB, 2, P], BF16)
        ctx_sb = sb("ctx_sb", [P, 2, T])
        ctx_in = sb("ctx_in", [P, NC, T])
        sum_in = sb("sum_in", [P, NC, T])
        x2 = sb("x2", [P, TB, D])
        x2T = sb("x2T", [P, NC, T + 1])
        mixk = sb("mixk", [P, NC, T])
        mixr = xnT
        hidden = sb("hidden", [P, NC, T])
        gate = sb("gate", [P, 2, T])
        ident = sb("ident", [P, P])
        ident_b = sb("ident_b", [P, P], BF16)
        mask_q = sb("mask_q", [P, P], BF16)
        mask_k = sb("mask_k", [P, P], BF16)

        scores = psum("scores", [P, RING, T])
        work = psum("work", [P, RING, T])
        ctx_ps = psum("ctx_ps", [P, 2, T])

        consts_ready = sem("consts_ready")
        ones_ready = sem("ones_ready")
        key_ones = sem("key_ones")
        one_minus_ready = sem("one_minus_ready")
        w_loaded = {name: sem(f"{name}_loaded") for name in w}
        mu_loaded = sem("mu_loaded")
        x_loaded = [sem(f"x_loaded{i}") for i in range(2)]
        ln_stats = sem("ln_stats")
        norm_ready = sem("norm_ready")
        xn_ready = sem("xn_ready")
        xT_ready = sem("xT_ready")
        high_ready = sem("high_ready")
        rest_ready = sem("rest_ready")
        parts_ready = sem("parts_ready")
        parts_stored = [sem(f"parts_stored{i}") for i in range(2)]
        v_ready = sem("v_ready")
        v_stored = sem("v_stored")
        k_loaded = [sem(f"k_loaded{i}") for i in range(KSLOTS)]
        v_loaded = [sem(f"v_loaded{i}") for i in range(KSLOTS)]
        q_loaded = [sem(f"q_loaded{i}") for i in range(QSLOTS)]
        m_loaded = [sem(f"m_loaded{i}") for i in range(QSLOTS)]
        max_done = sem("max_done")
        neg_max_ready = sem("neg_max_ready")
        max_parts_ready = sem("max_parts_ready")
        max_turned_ready = sem("max_turned_ready")
        scores_ready = sem("scores_ready")
        work_ready = sem("work_ready")
        probs_ready = sem("probs_ready")
        values_done = sem("values_done")
        ctx_ready = sem("ctx_ready")
        ctx_stored = [sem(f"ctx_stored{i}") for i in range(2)]
        ctx_loaded = sem("ctx_loaded")
        recip_ready = sem("recip_ready")
        ctx_normed = sem("ctx_normed")
        x2_ready = sem("x2_ready")
        mix_prev = sem("mix_prev")
        mix_ready = sem("mix_ready")
        last_token_kept = sem("last_token_kept")
        relu_ready = sem("relu_ready")
        hidden_ready = sem("hidden_ready")
        exp_gate_ready = sem("exp_gate_ready")
        gate_clamped = sem("gate_clamped")
        gate_plus1 = sem("gate_plus1")
        gate_ready = sem("gate_ready")
        y_ready = sem("y_ready")
        out_ready = sem("out_ready")
        out_stored = sem("out_stored")
        dve_chain = sem("dve_chain")
        pool_chain = sem("pool_chain")

        released_by = {"max": max_done, "turn_max": max_turned_ready, "turn": xT_ready,
                       "key": rest_ready, "query": rest_ready, "value": v_ready,
                       "attn_out": x2_ready, "up": relu_ready, "gate": gate_clamped, "down": y_ready}
        last_prologue_unit = {j: max(unit_of[s] for s in units if s[0] in ("key", "query", "value") and s[1] == j)
                              for j in range(NT)}
        q_step = {n: ("query", tile_of(n), half_of(n)) for n in range(GROUPS)}

        def stored_parts(eng, step):
            i = number[step]
            eng.wait_ge(parts_stored[i % 2], 16 * (i // 2 + 1))

        def slot_loads(half, c):
            return sum(kslot(a, b) == kslot(half, c) for a in range(half + 1) for b in range(NT)
                       if (a, b) <= (half, c))

        block = ctx.enter_context(nc.Block())

        @block.sync
        def _(sp):
            x_tiles = x.rearrange("(j i p) c -> j p i c", p=P, i=TB)
            out_tiles = out.rearrange("(j i p) c -> j p i c", p=P, i=TB)

            def load_w(name, src):
                sp.dma_start(w[name][:], src.rearrange("(c p) o -> p c o", p=P)).then_inc(w_loaded[name], 16)

            late = False
            for step in plan:
                kind = step[0]
                if kind == "x_load":
                    k = step[1]
                    if 2 <= k < NT + 2:
                        sp.wait_ge(xn_ready, k - 1)
                    elif k >= 2:
                        sp.wait_ge(x2_ready, 2 * (k - 1 - NT))
                    sp.dma_start(x_in[:, k % 2], x_tiles[k % NT]).then_inc(x_loaded[k % 2], 16)
                    if k == 0:
                        load_w("wk", wk_t)
                        load_w("wq", wq_t)
                        load_w("wv", wv_t)
                elif kind in ("key", "query"):
                    _, j, oc = step
                    i = number[step]
                    sp.wait_ge(parts_ready, i + 1)
                    dst = (k_parts if kind == "key" else q_parts)[:, P * oc:P * (oc + 1), T * j:T * (j + 1)]
                    sp.dma_start(dst.rearrange("r p t -> p r t"), parts[:, i % 2]).then_inc(parts_stored[i % 2], 16)
                elif kind == "key_load":
                    _, half, j = step
                    stored_parts(sp, ("key", j, half))
                    if half and j:
                        sp.wait_ge(scores_ready, GH * half0_blocks)
                    src = k_parts[:, P * half:P * (half + 1), T * j:T * (j + 1)].rearrange("r (h d) t -> r d h t", d=DK)
                    s = kslot(half, j)
                    for b, part in enumerate(KPARTS):
                        sp.dma_start(keys[DK * b:DK * (b + 1), s], src[part]).then_inc(k_loaded[s], 16)
                elif kind == "query_load":
                    n = step[1]
                    stored_parts(sp, q_step[n])
                    if n >= QSLOTS:
                        sp.wait_ge(scores_ready, GH * (last_block[n - QSLOTS] + 1))
                    j, r0 = tile_of(n), GH * DK * (2 * half_of(n) + n % 2)
                    src = q_parts[:, r0:r0 + GH * DK, T * j:T * (j + 1)].rearrange("r (h d) t -> r d h t", d=DK)
                    for b, part in enumerate(QPARTS):
                        sp.dma_start(queries[DK * b:DK * (b + 1), n % QSLOTS], src[part])\
                            .then_inc(q_loaded[n % QSLOTS], 16)
                elif kind == "value_store":
                    j = step[1]
                    sp.wait_ge(v_ready, 2 * (j + 1))
                    sp.dma_start(v_other[j], v_out[:].rearrange("p a v -> p (a v)")).then_inc(v_stored, 16)
                    if not late:
                        late = True
                        for name, src in (("wo", wo_t), ("wr", wr_t), ("wkf", wkf_t), ("wvf", wvf_t)):
                            load_w(name, src)
                        sp.dma_start(mu[:, 0], mu_k).then_inc(mu_loaded, 16)
                        sp.dma_start(mu[:, 1], mu_r).then_inc(mu_loaded, 16)
                elif kind == "value_load":
                    j = step[1]
                    sp.wait_ge(v_stored, 16 * NT)
                    sp.wait_ge(ones_ready, 3)
                    if j:
                        sp.wait_ge(values_done, half0_blocks)
                    s = kslot(1, j)
                    sp.dma_start(values[:, s].rearrange("p a v -> p (a v)"), v_other[j]).then_inc(v_loaded[s], 16)
                elif kind == "turn_max":
                    n = step[1]
                    sp.wait_ge(max_turned_ready, n + 1)
                    for r in range(3):
                        dst = queries[KR + r:KR + r + 1, n % QSLOTS].rearrange("o h (a q) -> o (h a) q", q=P)
                        sp.dma_start(dst, max_turned[GH * TB * r:GH * TB * (r + 1), n % 2])\
                            .then_inc(m_loaded[n % QSLOTS], 16)
                elif kind == "ctx_out":
                    n = step[1]
                    sp.wait_ge(ctx_ready, n + 1)
                    j, h0 = tile_of(n), HALF * half_of(n) + GH * (n % 2)
                    for i in range(GH):
                        sp.dma_start(ctx_dram[DK * (h0 + i):DK * (h0 + i + 1), T * j:T * (j + 1)],
                                     ctx_sb[32 * i:32 * i + DK, n % 2]).then_inc(ctx_stored[n % 2], 16)
                        sp.dma_start(sum_dram[h0 + i:h0 + i + 1, T * j:T * (j + 1)],
                                     ctx_sb[32 * i + DK:32 * i + DK + 1, n % 2]).then_inc(ctx_stored[n % 2], 16)
                elif kind == "ctx_load":
                    j = step[1]
                    for g in range(2):
                        sp.wait_ge(ctx_stored[g], 128 * (NT + j + 1))
                    if j:
                        sp.wait_ge(work_ready, unit_of["attn_out", j - 1, 1] + 1)
                        sp.wait_ge(ctx_normed, j)
                    sp.dma_start(ctx_in[:], ctx_dram[:, T * j:T * (j + 1)].rearrange("(c p) t -> p c t", p=P))\
                        .then_inc(ctx_loaded, 16)
                    for h in range(H):
                        p0 = DK * (h % HALF)
                        sp.dma_start(sum_in[p0:p0 + DK, h // HALF],
                                     sum_dram[h:h + 1, T * j:T * (j + 1)].broadcast_to([DK, T])).then_inc(ctx_loaded, 16)
                elif kind == "out_store":
                    j = step[1]
                    sp.wait_ge(out_ready, 2 * (j + 1))
                    sp.dma_start(out_tiles[j], x2[:]).then_inc(out_stored, 16)
            sp.wait_ge(out_stored, 16 * NT)

        @block.gpsimd
        def _(pool):
            chain = [0]

            def link(ins):
                chain[0] += 1
                ins.then_inc(pool_chain, 1)
                pool.wait_ge(pool_chain, chain[0])

            nc.gpsimd.memset(ident[:], 0.0).then_inc(pool_chain, 1)
            nc.gpsimd.memset(ident_b[:], 0.0).then_inc(pool_chain, 1)
            nc.gpsimd.memset(mask_q[:], 0.0).then_inc(pool_chain, 1)
            nc.gpsimd.memset(mask_k[:], 0.0).then_inc(pool_chain, 1)
            nc.gpsimd.memset(minus_half[:], -0.5).then_inc(pool_chain, 1)
            chain[0] = 5
            pool.wait_ge(pool_chain, 5)
            for m in (ident, ident_b):
                nc.gpsimd.affine_select(out=m[:], in_=m[:], compare_op=ALU.not_equal, fill=1.0, base=0,
                                        pattern=[[-1, P]], channel_multiplier=1).then_inc(consts_ready, 1)
            nc.gpsimd.affine_select(out=mask_q[:], in_=mask_q[:], compare_op=ALU.is_ge, fill=NEG, base=0,
                                    pattern=[[-1, P]], channel_multiplier=1).then_inc(consts_ready, 1)
            nc.gpsimd.affine_select(out=mask_k[:], in_=mask_k[:], compare_op=ALU.is_ge, fill=NEG, base=0,
                                    pattern=[[1, P]], channel_multiplier=-1).then_inc(consts_ready, 1)
            nc.gpsimd.memset(v_out[:], 1.0).then_inc(ones_ready, 1)
            nc.gpsimd.memset(values[:], 1.0).then_inc(ones_ready, 1)
            nc.gpsimd.memset(x2T[:, :, 0:1], 0.0).then_inc(ones_ready, 1)
            for step in plan:
                kind = step[0]
                if kind == "ln":
                    l = step[1]
                    pool.wait_ge(ln_stats, l + 1)
                    if l >= 2:
                        pool.wait_ge(xn_ready, l - 1)
                    link(nc.gpsimd.tensor_tensor(norm[:, l % 2, 0], var_mean[:, 0], minus_half[:], ALU.pow))
                    nc.gpsimd.tensor_tensor(norm[:, l % 2, 1], var_mean[:, 1], norm[:, l % 2, 0], ALU.mult)\
                        .then_inc(norm_ready, 1)
                elif kind in ("key", "query"):
                    i = number[step]
                    pool.wait_ge(rest_ready, i + 1)
                    link(nc.gpsimd.tensor_scalar(parts[:, i % 2, 1], rest[:, i % 2], 1.0, 1.0, ALU.mult, ALU.mult))
                    nc.gpsimd.tensor_tensor(parts[:, i % 2, 2], rest[:, i % 2], parts[:, i % 2, 1],
                                            ALU.subtract).then_inc(parts_ready, 1)
                elif kind == "negmax":
                    n = step[1]
                    pool.wait_ge(neg_max_ready, n + 1)
                    if n >= 2:
                        pool.wait_ge(work_ready, unit_of["turn_max", n - 2] + 1)
                    m, mp = neg_max[:, n % 2], max_parts[:, n % 2]
                    link(nc.gpsimd.tensor_scalar(mp[:, 0], m, 1.0, 1.0, ALU.mult, ALU.mult))
                    link(nc.gpsimd.tensor_tensor(max_rest[:], m, mp[:, 0], ALU.subtract))
                    link(nc.gpsimd.tensor_scalar(mp[:, 1], max_rest[:], 1.0, 1.0, ALU.mult, ALU.mult))
                    nc.gpsimd.tensor_tensor(mp[:, 2], max_rest[:], mp[:, 1], ALU.subtract)\
                        .then_inc(max_parts_ready, 1)
                elif kind == "attn_norm":
                    pool.wait_ge(recip_ready, step[1] + 1)
                    pool.wait_ge(ctx_loaded, 16 * (1 + H) * (step[1] + 1))
                    nc.gpsimd.tensor_tensor(ctx_in[:], ctx_in[:], sum_in[:], ALU.mult).then_inc(ctx_normed, 1)
                elif kind == "mix":
                    j = step[1]
                    pool.wait_ge(xT_ready, NC * (NT + j + 1))
                    if j == 0:
                        pool.wait_ge(one_minus_ready, 1)
                        pool.wait_ge(ones_ready, 3)
                        pool.wait_ge(work_ready, last_prologue_unit[NT - 1] + 1)
                    else:
                        pool.wait_ge(work_ready, unit_of["gate", j - 1, 1] + 1)
                    for a, m in enumerate((mixk, mixr)):
                        for c in range(NC):
                            nc.gpsimd.tensor_scalar(m[:, c], x2T[:, c, 0:T], one_minus_mu[:, a, c:c + 1], 1.0,
                                                    ALU.mult, ALU.mult).then_inc(mix_prev, 1)
                elif kind == "up":
                    oc = step[2]
                    pool.wait_ge(relu_ready, number[step] + 1)
                    nc.gpsimd.tensor_tensor(hidden[:, oc], hidden[:, oc], hidden[:, oc], ALU.mult)\
                        .then_inc(hidden_ready, 1)
                elif kind == "gate":
                    i2 = step[2]
                    pool.wait_ge(exp_gate_ready, number[step] + 1)
                    nc.gpsimd.tensor_scalar(gate[:, i2], gate[:, i2], 1.0, 1.0, ALU.add, ALU.mult)\
                        .then_inc(gate_plus1, 1)
                elif kind == "down":
                    i2 = step[2]
                    pool.wait_ge(y_ready, number[step] + 1)
                    xo = x2[:, 2 * i2:2 * i2 + 2].rearrange("p a c -> p (a c)")
                    nc.gpsimd.tensor_tensor(xo, xo, gate[:, i2], ALU.add).then_inc(out_ready, 1)

        @block.scalar
        def _(act):
            s = 0
            for step in plan:
                kind = step[0]
                u = unit_of.get(step)
                if kind == "keys":
                    _, n, kb = step
                    cols = T - P * max(0, kb - TB * tile_of(n))
                    for i in range(GH):
                        act.wait_ge(scores_ready, s + 1)
                        if s >= PSLOTS:
                            act.wait_ge(values_done, (s - PSLOTS) // GH + 1)
                        nc.scalar.activation(probs[:, s % PSLOTS, 0:cols], scores[:, s % RING, 0:cols], ACT.Exp)\
                            .then_inc(probs_ready, 1)
                        s += 1
                elif kind == "ctx_out":
                    n = step[1]
                    act.wait_ge(values_done, last_block[n] + 1)
                    if n >= 2:
                        act.wait_ge(ctx_stored[n % 2], 128 * (n // 2))
                    nc.scalar.copy(ctx_sb[:, n % 2], ctx_ps[:, n % 2]).then_inc(ctx_ready, 1)
                elif kind == "ln":
                    l = step[1]
                    act.wait_ge(norm_ready, l + 1)
                    if l:
                        act.wait_ge(work_ready, unit_of["turn", l - 1, NC - 1] + 1)
                    src = x_in[:, l % 2] if l < NT else x2
                    for i in range(TB):
                        last = nc.scalar.activation(xn[:, i], src[:, i], ACT.Identity,
                                                    bias=norm[:, l % 2, 1, i:i + 1], scale=norm[:, l % 2, 0, i:i + 1])
                    last.then_inc(xn_ready, 1)
                elif kind == "turn":
                    _, l, c = step
                    if l < NT:
                        if l:
                            act.wait_ge(work_ready, last_prologue_unit[l - 1] + 1)
                        dst = xnT[:, c]
                    else:
                        if l > NT:
                            act.wait_ge(mix_ready, 4 * (l - NT))
                            act.wait_ge(xT_ready, NC * l)
                            nc.scalar.copy(x2T[:, c, 0:1], x2T[:, c, T:T + 1]).then_inc(last_token_kept, 1)
                            act.wait_ge(last_token_kept, NC * (l - NT - 1) + c + 1)
                        dst = x2T[:, c, 1:T + 1]
                    act.wait_ge(work_ready, u + 1)
                    nc.scalar.copy(dst, work[:, u % RING]).then_inc(xT_ready, 1)
                elif kind in ("key", "query"):
                    i = number[step]
                    act.wait_ge(work_ready, u + 1)
                    if i >= 2:
                        act.wait_ge(parts_stored[i % 2], 16 * (i // 2))
                    nc.scalar.mul(parts[:, i % 2, 0], work[:, u % RING], 1.0 if kind == "key" else DK ** -0.5)\
                        .then_inc(high_ready, 1)
                elif kind == "value":
                    _, j, i2 = step
                    act.wait_ge(work_ready, u + 1)
                    act.wait_ge(ones_ready, 2)
                    if j:
                        act.wait_ge(v_stored, 16 * j)
                    src = work[:, u % RING].rearrange("p (a f h d) -> p a f h d", a=2, f=2, d=DK)
                    for f, dst in enumerate((values[:, j], v_out)):
                        d4 = dst[:, 2 * i2:2 * i2 + 2, 0:HALF * VW].rearrange("p a (h v) -> p a h v", v=VW)
                        for a in range(2):
                            last = nc.scalar.copy(d4[:, a, :, 0:DK], src[:, a, f])
                    last.then_inc(v_ready, 1)
                elif kind == "turn_max":
                    n = step[1]
                    act.wait_ge(work_ready, u + 1)
                    if n >= 2:
                        act.wait_ge(m_loaded[(n - 2) % QSLOTS], 48 * ((n - 2) // QSLOTS + 1))
                    nc.scalar.copy(max_turned[:, n % 2], work[0:3 * GH * TB, u % RING].bitcast(BF16)[:, 0:P])\
                        .then_inc(max_turned_ready, 1)
                elif kind == "up":
                    _, j, oc = step
                    act.wait_ge(work_ready, u + 1)
                    if j:
                        act.wait_ge(work_ready, unit_of["down", j - 1, 1] + 1)
                    nc.scalar.activation(hidden[:, oc], work[:, u % RING], ACT.Relu).then_inc(relu_ready, 1)
                elif kind == "gate":
                    i2 = step[2]
                    act.wait_ge(gate_clamped, number[step] + 1)
                    nc.scalar.activation(gate[:, i2], gate[:, i2], ACT.Exp, scale=-1.0)\
                        .then_inc(exp_gate_ready, 1)

        @block.vector
        def _(dve):
            chain = [0]

            def link(ins):
                chain[0] += 1
                ins.then_inc(dve_chain, 1)
                dve.wait_ge(dve_chain, chain[0])

            def gate_reciprocals(j):
                for i2 in range(2):
                    dve.wait_ge(gate_plus1, 2 * j + i2 + 1)
                    nc.vector.reciprocal(gate[:, i2], gate[:, i2]).then_inc(gate_ready, 1)

            first_ln2 = True
            for step in plan:
                kind = step[0]
                u = unit_of.get(step)
                if kind == "max":
                    _, n, i, qt, p = step
                    cols = T if p < tile_of(n) else P * (qt + 1)
                    dve.wait_ge(work_ready, u + 1)
                    nc.vector.reduce_max(row_max[:, n % 2, TB * i + qt, p:p + 1], work[:, u % RING, 0:cols], AXX)\
                        .then_inc(max_done, 1)
                elif kind == "negmax":
                    n = step[1]
                    dve.wait_ge(max_done, max_through[n])
                    if n >= 2:
                        dve.wait_ge(max_parts_ready, n - 1)
                    nc.vector.tensor_reduce(neg_max[:, n % 2], row_max[:, n % 2, :, 0:tile_of(n) + 1], AXX, ALU.max,
                                            negate=True).then_inc(neg_max_ready, 1)
                elif kind == "ln":
                    l = step[1]
                    if l < NT:
                        dve.wait_ge(x_loaded[l % 2], 16 * (l // 2 + 1))
                    else:
                        dve.wait_ge(x2_ready, 2 * (l - NT + 1))
                    if l:
                        dve.wait_ge(norm_ready, l)
                    src = x_in[:, l % 2] if l < NT else x2
                    for slot in ([l] if l < NT - 1 else [l, l + 1] if l == NT - 1 else []):
                        nc.vector.memset(keys[KR:KM, slot].rearrange("p h t -> p (h t)").bitcast(U32), 0x3F803F80)\
                            .then_inc(key_ones, 1)
                    for i in range(TB):
                        last = nc.vector.bn_stats(bn[:, i], src[:, i])
                    link(last)
                    for i in range(TB):
                        last = nc.vector.bn_aggr(mean_var[:, i], bn[:, i])
                    link(last)
                    nc.vector.tensor_scalar(var_mean[:, 0], mean_var[:, :, 1], EPS, None, ALU.add)
                    nc.vector.tensor_scalar(var_mean[:, 1], mean_var[:, :, 0], -1.0, None, ALU.mult)\
                        .then_inc(ln_stats, 1)
                elif kind in ("key", "query"):
                    i = number[step]
                    dve.wait_ge(high_ready, i + 1)
                    if i >= 2:
                        dve.wait_ge(parts_ready, i - 1)
                    nc.vector.scalar_tensor_tensor(out=rest[:, i % 2], in0=work[:, u % RING],
                                                   scalar=1.0 if kind == "key" else DK ** -0.5,
                                                   in1=parts[:, i % 2, 0], op0=ALU.mult, op1=ALU.subtract)\
                        .then_inc(rest_ready, 1)
                elif kind == "attn_norm":
                    dve.wait_ge(ctx_loaded, 16 * (1 + H) * (step[1] + 1))
                    nc.vector.reciprocal(sum_in[:], sum_in[:]).then_inc(recip_ready, 1)
                elif kind == "attn_out":
                    _, j, i2 = step
                    dve.wait_ge(work_ready, u + 1)
                    dve.wait_ge(x_loaded[j % 2], 16 * ((NT + j) // 2 + 1))
                    if j:
                        dve.wait_ge(out_stored, 16 * j)
                    nc.vector.tensor_tensor(x2[:, 2 * i2:2 * i2 + 2],
                                            work[:, u % RING].rearrange("p (a c) -> p a c", a=2),
                                            x_in[:, j % 2, 2 * i2:2 * i2 + 2], ALU.add).then_inc(x2_ready, 1)
                elif kind == "mix":
                    j = step[1]
                    if first_ln2:
                        first_ln2 = False
                        dve.wait_ge(mu_loaded, 32)
                        nc.vector.tensor_scalar(one_minus_mu[:], mu[:], -1.0, 1.0, ALU.mult, ALU.add)\
                            .then_inc(one_minus_ready, 1)
                    for a, m in enumerate((mixk, mixr)):
                        for c in range(NC):
                            dve.wait_ge(mix_prev, 4 * j + 2 * a + c + 1)
                            nc.vector.scalar_tensor_tensor(out=m[:, c], in0=x2T[:, c, 1:T + 1],
                                                           scalar=mu[:, a, c:c + 1], in1=m[:, c],
                                                           op0=ALU.mult, op1=ALU.add).then_inc(mix_ready, 1)
                elif kind == "gate":
                    _, j, i2 = step
                    dve.wait_ge(work_ready, u + 1)
                    if j:
                        dve.wait_ge(out_ready, 2 * j)
                    nc.vector.tensor_scalar(gate[:, i2], work[:, u % RING], GATE_MIN, None, ALU.max)\
                        .then_inc(gate_clamped, 1)
                elif kind == "down":
                    _, j, i2 = step
                    if i2 == 0:
                        gate_reciprocals(j)
                    dve.wait_ge(work_ready, u + 1)
                    dve.wait_ge(gate_ready, number[step] + 1)
                    nc.vector.tensor_tensor(gate[:, i2], work[:, u % RING], gate[:, i2], ALU.mult)\
                        .then_inc(y_ready, 1)

        @block.tensor
        def _(pe):
            def own_bank(u):
                if u >= RING:
                    before = units[u - RING]
                    pe.wait_ge(released_by[before[0]], number[before] + 1)
                return work[:, u % RING]

            def values_product(n, kb):
                off = P * max(0, kb - TB * tile_of(n))
                g = block_of[n, kb]
                half, c = half_of(n), kb // TB
                pe.wait_ge(probs_ready, GH * (g + 1))
                if kb == 0 and n >= 2:
                    pe.wait_ge(ctx_ready, n - 1)
                if half == 0 and kb % TB == 0:
                    pe.wait_ge(v_ready, 2 * (c + 1))
                elif half == 1:
                    pe.wait_ge(v_loaded[kslot(1, c)], 16)
                for i in range(GH):
                    v0 = VW * (GH * (n % 2) + i)
                    last = nc.tensor.matmul(ctx_ps[32 * i:32 * i + 32, n % 2, off:T],
                                            values[:, kslot(half, c), kb % TB, v0:v0 + 32],
                                            probs[:, (GH * g + i) % PSLOTS, 0:T - off],
                                            start=(kb == 0), stop=(kb == TB * (tile_of(n) + 1) - 1),
                                            tile_position=(0, 32 * i))
                last.then_inc(values_done, 1)

            pe.wait_ge(consts_ready, 4)
            pending = []
            for step in plan:
                kind = step[0]
                u = unit_of.get(step)
                if kind == "keys":
                    _, n, kb = step
                    j, half = tile_of(n), half_of(n)
                    off = P * max(0, kb - TB * j)
                    slot = kslot(half, kb // TB)
                    if kb == 0:
                        pe.wait_ge(m_loaded[n % QSLOTS], 48 * (n // QSLOTS + 1))
                    pe.wait_ge(key_ones, slot + 1)
                    pe.wait_ge(k_loaded[slot], 16 * BANDS * slot_loads(half, kb // TB))
                    for i in range(GH):
                        s = GH * block_of[n, kb] + i
                        if s >= RING:
                            pe.wait_ge(probs_ready, s - RING + 1)
                        last = nc.tensor.matmul(scores[:, s % RING, 0:T - off],
                                                keys[0:KM, slot, GH * (n % 2) + i, P * (kb % TB):P * (kb % TB + 1)],
                                                queries[0:KM, n % QSLOTS, i, off:T], start=True, stop=(kb < TB * j))
                        if kb >= TB * j:
                            last = nc.tensor.matmul(scores[:, s % RING, 0:P], ident_b[:], mask_k[:],
                                                    start=False, stop=True)
                        last.then_inc(scores_ready, 1)
                    if pending:
                        values_product(*pending.pop())
                    pending.append((n, kb))
                elif kind == "ctx_out":
                    if pending and pending[0][0] == step[1]:
                        values_product(*pending.pop())
                elif kind == "max":
                    _, n, i, qt, p = step
                    half = half_of(n)
                    cols = T if p < tile_of(n) else P * (qt + 1)
                    pe.wait_ge(q_loaded[n % QSLOTS], 16 * BANDS * (n // QSLOTS + 1))
                    pe.wait_ge(k_loaded[kslot(half, p)], 16 * BANDS * slot_loads(half, p))
                    bank = own_bank(u)
                    last = nc.tensor.matmul(bank[:, 0:cols], queries[0:KR, n % QSLOTS, i, P * qt:P * (qt + 1)],
                                            keys[0:KR, kslot(half, p), GH * (n % 2) + i, 0:cols],
                                            start=True, stop=(p < tile_of(n)))
                    if p == tile_of(n):
                        last = nc.tensor.matmul(bank[:, cols - P:cols], ident_b[:], mask_q[:], start=False, stop=True)
                    last.then_inc(work_ready, 1)
                elif kind == "turn_max":
                    n = step[1]
                    pe.wait_ge(max_parts_ready, n + 1)
                    bank = own_bank(u)
                    nc.tensor.transpose(bank[0:3 * GH * TB].bitcast(BF16)[:, 0:P],
                                        max_parts[:, n % 2].rearrange("p r m -> p (r m)"), ident_b[:])\
                        .then_inc(work_ready, 1)
                elif kind == "turn":
                    _, l, c = step
                    pe.wait_ge(xn_ready, l + 1)
                    bank = own_bank(u)
                    for i in range(TB):
                        last = nc.tensor.transpose(bank[:, P * i:P * (i + 1)], xn[:, i, P * c:P * (c + 1)], ident[:])
                    last.then_inc(work_ready, 1)
                elif kind in ("key", "query", "up"):
                    _, j, oc = step
                    if kind == "up":
                        pe.wait_ge(mix_ready, 4 * j + 2)
                    else:
                        pe.wait_ge(xT_ready, NC * (j + 1))
                    name = {"key": "wk", "query": "wq", "up": "wkf"}[kind]
                    if j == 0:
                        pe.wait_ge(w_loaded[name], 16)
                    rhs = mixk if kind == "up" else xnT
                    bank = own_bank(u)
                    for c in range(NC):
                        last = nc.tensor.matmul(bank, w[name][:, c, P * oc:P * (oc + 1)], rhs[:, c],
                                                start=(c == 0), stop=(c == NC - 1))
                    last.then_inc(work_ready, 1)
                elif kind in ("value", "attn_out", "gate", "down"):
                    _, j, i2 = step
                    if kind == "value":
                        pe.wait_ge(xT_ready, NC * (j + 1))
                    elif kind == "attn_out":
                        pe.wait_ge(ctx_normed, j + 1)
                    elif kind == "gate":
                        pe.wait_ge(mix_ready, 4 * (j + 1))
                    else:
                        pe.wait_ge(hidden_ready, 2 * (j + 1))
                    name, lhs = {"value": ("wv", xnT), "attn_out": ("wo", ctx_in), "gate": ("wr", mixr),
                                 "down": ("wvf", hidden)}[kind]
                    if j == 0:
                        pe.wait_ge(w_loaded[name], 16)
                    bank = own_bank(u)
                    for a in range(2):
                        t0 = P * (2 * i2 + a)
                        for c in range(NC):
                            last = nc.tensor.matmul(bank[:, D * a:D * (a + 1)], lhs[:, c, t0:t0 + P], w[name][:, c],
                                                    start=(c == 0), stop=(c == NC - 1))
                    last.then_inc(work_ready, 1)


def kernel(L0_attn_x, L0_attn_wq, L0_attn_wk, L0_attn_wv, L0_attn_wo, L0_ffn_W_r, L0_ffn_W_k, L0_ffn_W_v,
           L0_ffn_mu_r, L0_ffn_mu_k):
    import numpy as np
    import concourse.bacc as bacc
    from concourse.bass_utils import run_bass_kernel_spmd

    x = np.asarray(L0_attn_x)
    laid_out = {"x": x.reshape(x.shape[1], x.shape[2])}
    for name, weight in (("wq_t", L0_attn_wq), ("wk_t", L0_attn_wk), ("wv_t", L0_attn_wv), ("wo_t", L0_attn_wo),
                         ("wr_t", L0_ffn_W_r), ("wkf_t", L0_ffn_W_k), ("wvf_t", L0_ffn_W_v)):
        laid_out[name] = np.ascontiguousarray(np.asarray(weight).T)
    for name, mix in (("mu_r", L0_ffn_mu_r), ("mu_k", L0_ffn_mu_k)):
        laid_out[name] = np.ascontiguousarray(np.asarray(mix).reshape(NC, P).T)
    nc = bacc.Bacc("TRN2", target_bir_lowering=False, num_devices=1)
    args = {name: nc.dram_tensor(name, a.shape, mybir.dt.from_np(a.dtype), kind="ExternalInput").ap()
            for name, a in laid_out.items()}
    out = nc.dram_tensor("out", (S, D), F32, kind="ExternalOutput").ap()
    attention_ffn(nc, out=out, **args)
    result = run_bass_kernel_spmd(nc, [laid_out], core_ids=[0])
    return result.results[0]["out"].reshape(x.shape)
```

```python
from contextlib import ExitStack

import concourse.bass as bass
from concourse import mybir

ALU = mybir.AluOpType
ACT = mybir.ActivationFunctionType
AXX = mybir.AxisListType.X
F32 = mybir.dt.float32
BF16 = mybir.dt.bfloat16
U32 = mybir.dt.uint32

P = 128
S, D, H = 4096, 256, 16
DK = D // H
T = 512
NT = S // T
TB = T // P
NC = D // P
HALF = H // 2
GH = 4
GROUPS = 2 * NT * 2
KSLOTS = NT + 1
QSLOTS = 4
PSLOTS = 8
RING = 3
SRING = 4
CBANKS = 1
VW = DK + 1
VP = 152
EPS = 1e-5
NEG = -1e30
LOWEST = -3e38
RUNS = ((0, (0, 1, 2), (0, 0, 0)), (3, (0, 1), (1, 1)), (5, (0,), (2,)))
BANDS = sum(len(parts) for _, parts, _ in RUNS)
KR = BANDS * DK
KM = KR + 3


LEAD = 18.0


def tile_of(n):
    return n % (2 * NT) // 2


def half_of(n):
    return n // (2 * NT)


def kslot(half, c):
    return (NT * half + c) % KSLOTS


def block_dur(n, kb):
    return 2.638 * (T - P * max(0, kb - TB * tile_of(n))) / T + 0.2


def pace_attention(gap):
    at, start, end, now = [], {}, {}, 0.0
    for n in range(GROUPS):
        now += gap[n]
        start[n] = now
        for kb in range(TB * (tile_of(n) + 1)):
            dur = block_dur(n, kb)
            for i in range(GH):
                at.append((now + dur * i / GH, ("score", n, kb, i)))
                if kb >= TB * tile_of(n):
                    at.append((now + dur * i / GH + 0.069, ("mask", n, kb, i)))
            if kb >= TB * tile_of(n):
                due_values = now + max(1.6 * dur, 2.5)
            else:
                due_values = now + 1.6 * dur
            last = kb == TB * (tile_of(n) + 1) - 1
            following = 9.0 if last and n == GROUPS - 1 else block_dur(n + 1, 0) if last else block_dur(n, kb + 1)
            at.append((min(due_values, now + dur + following), ("probs_values", n, kb)))
            now += dur
        end[n] = now
        at.append((now + 1.619, ("ctx_out", n)))
    row_maxima, first_max, due = {}, {}, None
    for n in reversed(range(GROUPS)):
        due = start[n] - LEAD if due is None else min(due, start[n] - LEAD)
        steps = [(due + 6.0, ("turn_max", n)), (due + 0.01, ("negmax", n))]
        for i in reversed(range(GH)):
            for qt in reversed(range(TB)):
                for p in reversed(range(tile_of(n) + 1)):
                    w = T if p < tile_of(n) else P * (qt + 1)
                    due -= 0.10 + 0.54 * w / T
                    steps.append((due, ("max", n, i, qt, p)))
        row_maxima[n], first_max[n] = steps[::-1], due
    for n in range(GROUPS):
        free = end[n - QSLOTS] + 0.2 if n >= QSLOTS else -1e9
        if n >= 2 * KSLOTS:
            free = max(free, end[2 * NT - 1] + 3.0)
        if n:
            free = max(free, row_maxima[n - 1][-2][0] + 0.01)
        shift = max(0.0, free - first_max[n])
        row_maxima[n] = [(t + shift, step) for t, step in row_maxima[n]]
        first_max[n] += shift
        late = row_maxima[n][-1][0] - start[n]
        if late > 0:
            return n, late, None, None, None
        at += row_maxima[n]
        at.append((max(first_max[n] - 10.676, end[n - QSLOTS] + 0.1 if n >= QSLOTS else -1e9), ("query_load", n)))
    return None, 0.0, at, first_max, end


def make_plan():
    gap = [0.0] * GROUPS
    n, late, at, first_max, end = pace_attention(gap)
    while at is None:
        gap[n] += late + 0.5
        n, late, at, first_max, end = pace_attention(gap)
    b = -1e9
    for j in range(NT):
        b = max(b + 16.816, first_max[2 * j] - (26.546 if j == 0 else 27.0))
        at += [(b - 19.241, ("x_load", j)), (b - 13.602, ("ln", j)), (b - 7.693, ("normalize", j)),
               (b, ("turn", j, 0)), (b + 1.0, ("turn", j, 1)),
               (b + 3.85, ("key", j, 0)), (b + 6.0, ("query", j, 0)),
               (b + 6.279, ("value", j, 0)), (b + 8.552, ("value", j, 1)), (b + 10.0, ("key_load", 0, j)),
               (b + 11.0, ("value_store", j)), (b + 12.886, ("key", j, 1)), (b + 14.0, ("query", j, 1))]
        t = first_max[2 * NT + 2 * j] - 12.0
        if j:
            t = max(t, end[2 * NT - 1] + 0.1)
        at += [(t, ("key_load", 1, j)), (t + 0.1, ("value_load", j))]
        for half in range(2):
            t = end[2 * NT * half + 2 * j + 1] + 4.851
            at += [(t, ("sums_load", half, j)), (t + 6.863, ("sums", half, j)), (t + 7.0, ("sums_store", half, j))]
    t = 0.0
    for j in range(NT):
        t = max(t, end[2 * NT + 2 * j + 1] + 12.0)
        at += [(t, ("ctx_load", j)), (t, ("x_load", NT + j)), (t + 8.421, ("attn_norm", j)),
               (t + 13.938, ("attn_out", j, 0)), (t + 16.254, ("attn_out", j, 1)),
               (t + 18.591, ("ln", NT + j)), (t + 22.236, ("normalize", NT + j)),
               (t + 28.565, ("turn", NT + j, 0)), (t + 29.0, ("turn", NT + j, 1)), (t + 31.175, ("mix", j)),
               (t + 32.439, ("up", j, 0)), (t + 34.501, ("up", j, 1)),
               (t + 38.356, ("gate", j, 0)), (t + 42.87, ("gate", j, 1)),
               (t + 44.133, ("down", j, 0)), (t + 44.682, ("down", j, 1)), (t + 51.0, ("out_store", j))]
        t += 40.0
    return [step for _, step in sorted(at, key=lambda a: a[0])]


WORK = ("max", "turn_max", "turn", "key", "query", "value", "attn_out", "up", "gate", "down")


def after_next_max(plan, kinds):
    order, held = [], []
    for step in plan:
        if step[0] in kinds:
            order += held
            held = [step]
        elif step[0] == "max":
            order += [step] + held
            held = []
        else:
            order += held + [step]
            held = []
    return order + held


def attention_ffn(nc, x, wq_t, wk_t, wv_t, wo_t, wr_t, wkf_t, wvf_t, mu_r, mu_k, out):
    plan = make_plan()

    number, count, unit_of, units = {}, {}, {}, []
    for step in plan:
        kind = "qk" if step[0] in ("key", "query") else step[0]
        number[step] = count.get(kind, 0)
        count[kind] = number[step] + 1
        if step[0] in WORK:
            unit_of[step] = len(units)
            units.append(step)
    block_of, n_blocks = {}, 0
    for n in range(GROUPS):
        for kb in range(TB * (tile_of(n) + 1)):
            block_of[n, kb] = n_blocks
            n_blocks += 1
    last_block = {n: block_of[n, TB * (tile_of(n) + 1) - 1] for n in range(GROUPS)}
    half0_blocks = last_block[2 * NT - 1] + 1
    max_through = {}
    for step in units:
        if step[0] == "max":
            max_through[step[1]] = number[step] + 1

    def dram(name, shape, dt):
        return nc.dram_tensor(name, shape, dt, kind="Internal").ap()

    q_bands = dram("q_bands", [2, BANDS, P, S], BF16)
    k_bands = dram("k_bands", [2, BANDS, P, S], BF16)
    v_other = dram("v_other", [NT, P, TB * VP], F32)
    ctx_dram = dram("ctx_dram", [32 * H, S], F32)
    recip_dram = dram("recip_dram", [2, HALF, S], F32)

    with ExitStack() as ctx:
        def sb(name, shape, dt=F32):
            return ctx.enter_context(nc.sbuf_tensor(name, shape, dt))

        def psum(name, shape):
            return ctx.enter_context(nc.psum_tensor(name, shape, F32))

        def sem(name):
            return ctx.enter_context(nc.semaphore(name))

        keys = sb("keys", [P, KSLOTS, HALF, T], BF16)
        queries = sb("queries", [P, QSLOTS, GH, T], BF16)
        values = sb("values", [P, KSLOTS, TB, VP])
        probs = sb("probs", [P, PSLOTS, T])
        w = {name: sb(name, [P, NC, D]) for name in ("wq", "wk", "wv", "wo", "wr", "wkf", "wvf")}
        mu = sb("mu", [P, 2, NC])
        one_minus_mu = sb("one_minus_mu", [P, 2, NC])
        x_in = sb("x_in", [P, 2, TB, D])
        xn = sb("xn", [P, TB, D])
        xnT = sb("xnT", [P, NC, T])
        parts = sb("parts", [P, 2, 3, T], BF16)
        rest = sb("rest", [P, 2, T])
        v_out = sb("v_out", [P, TB, VP])
        bn = sb("bn", [P, TB, 6])
        mean_var = sb("mean_var", [P, TB, 2])
        var_mean = sb("var_mean", [P, 2, TB])
        minus_half = sb("minus_half", [P, TB])
        norm = sb("norm", [P, 2, 2, TB])
        row_max = sb("row_max", [P, 2, GH * TB, NT])
        neg_max = sb("neg_max", [P, 2, GH * TB])
        max_rest = sb("max_rest", [P, GH * TB])
        max_parts = sb("max_parts", [P, 2, 3, GH * TB], BF16)
        max_turned = sb("max_turned", [3 * GH * TB, 2, P], BF16)
        ctx_sb = sb("ctx_sb", [P, 2, T])
        ctx_in = sb("ctx_in", [P, NC, T])
        recip_in = sb("recip_in", [P, NC, T])
        sums = sb("sums", [HALF * HALF, T // HALF])
        x2 = sb("x2", [P, TB, D])
        x2T = sb("x2T", [P, NC, T + 1])
        mixk = sb("mixk", [P, NC, T])
        mixr = xnT
        hidden = sb("hidden", [P, NC, T])
        gate = sb("gate", [P, 2, T])
        ident = sb("ident", [P, P])
        ident_b = sb("ident_b", [P, P], BF16)
        mask = sb("mask", [P, T], BF16)

        scores = psum("scores", [P, SRING, T])
        work = psum("work", [P, RING, T])
        ctx_ps = psum("ctx_ps", [P, CBANKS, T])

        consts_ready = sem("consts_ready")
        mask_made = sem("mask_made")
        ones_ready = sem("ones_ready")
        key_ones = sem("key_ones")
        one_minus_ready = sem("one_minus_ready")
        w_loaded = {name: sem(f"{name}_loaded") for name in w}
        mu_loaded = sem("mu_loaded")
        x_loaded = [sem(f"x_loaded{i}") for i in range(2)]
        ln_stats = sem("ln_stats")
        norm_ready = sem("norm_ready")
        xn_ready = sem("xn_ready")
        xT_ready = sem("xT_ready")
        high_ready = sem("high_ready")
        rest_ready = sem("rest_ready")
        parts_ready = sem("parts_ready")
        parts_stored = [sem(f"parts_stored{i}") for i in range(2)]
        v_ready = sem("v_ready")
        v_stored = sem("v_stored")
        k_loaded = [sem(f"k_loaded{i}") for i in range(KSLOTS)]
        v_loaded = [sem(f"v_loaded{i}") for i in range(KSLOTS)]
        q_loaded = [sem(f"q_loaded{i}") for i in range(QSLOTS)]
        m_loaded = [sem(f"m_loaded{i}") for i in range(QSLOTS)]
        max_done = sem("max_done")
        neg_max_ready = sem("neg_max_ready")
        max_parts_ready = sem("max_parts_ready")
        max_turned_ready = sem("max_turned_ready")
        scores_ready = sem("scores_ready")
        work_ready = sem("work_ready")
        probs_ready = sem("probs_ready")
        probs_masked = sem("probs_masked")
        values_done = sem("values_done")
        ctx_ready = sem("ctx_ready")
        ctx_stored = [sem(f"ctx_stored{i}") for i in range(2)]
        sums_loaded = sem("sums_loaded")
        sums_ready = sem("sums_ready")
        sums_stored = sem("sums_stored")
        ctx_loaded = sem("ctx_loaded")
        ctx_normed = sem("ctx_normed")
        x2_ready = sem("x2_ready")
        mix_prev = sem("mix_prev")
        mix_ready = sem("mix_ready")
        last_token_kept = sem("last_token_kept")
        relu_ready = sem("relu_ready")
        hidden_ready = sem("hidden_ready")
        tanh_ready = sem("tanh_ready")
        gate_ready = sem("gate_ready")
        y_ready = sem("y_ready")
        out_ready = sem("out_ready")
        out_stored = sem("out_stored")
        dve_chain = sem("dve_chain")
        pool_chain = sem("pool_chain")

        released_by = {"max": max_done, "turn_max": max_turned_ready, "turn": xT_ready,
                       "key": rest_ready, "query": rest_ready, "value": v_ready,
                       "attn_out": x2_ready, "up": relu_ready, "gate": tanh_ready, "down": y_ready}
        last_prologue_unit = {j: max(unit_of[s] for s in units if s[0] in ("key", "query", "value") and s[1] == j)
                              for j in range(NT)}
        q_step = {n: ("query", tile_of(n), half_of(n)) for n in range(GROUPS)}

        def stored_parts(eng, step):
            i = number[step]
            eng.wait_ge(parts_stored[i % 2], 16 * len(RUNS) * (i // 2 + 1))

        def slot_loads(half, c):
            return sum(kslot(a, b) == kslot(half, c) for a in range(half + 1) for b in range(NT)
                       if (a, b) <= (half, c))

        block = ctx.enter_context(nc.Block())

        @block.sync
        def _(sp):
            x_tiles = x.rearrange("(j i p) c -> j p i c", p=P, i=TB)
            out_tiles = out.rearrange("(j i p) c -> j p i c", p=P, i=TB)

            def load_w(name, src):
                sp.dma_start(w[name][:], src.rearrange("(c p) o -> p c o", p=P)).then_inc(w_loaded[name], 16)

            late = False
            for step in plan:
                kind = step[0]
                if kind == "x_load":
                    k = step[1]
                    if 2 <= k < NT + 2:
                        sp.wait_ge(xn_ready, k - 1)
                    elif k >= 2:
                        sp.wait_ge(x2_ready, 2 * (k - 1 - NT))
                    sp.dma_start(x_in[:, k % 2], x_tiles[k % NT]).then_inc(x_loaded[k % 2], 16)
                    if k == 0:
                        load_w("wk", wk_t)
                        load_w("wq", wq_t)
                        load_w("wv", wv_t)
                elif kind in ("key", "query"):
                    _, j, oc = step
                    i = number[step]
                    sp.wait_ge(parts_ready, i + 1)
                    for b, of_query, of_key in RUNS:
                        m = len(of_query)
                        if kind == "key":
                            src = parts[:, i % 2, of_key[0]:of_key[0] + 1].broadcast_to([P, m, T])
                        else:
                            src = parts[:, i % 2, 0:m]
                        dst = (k_bands if kind == "key" else q_bands)[oc, b:b + m, :, T * j:T * (j + 1)]
                        sp.dma_start(dst.rearrange("r p t -> p r t"), src).then_inc(parts_stored[i % 2], 16)
                elif kind == "key_load":
                    _, half, j = step
                    stored_parts(sp, ("key", j, half))
                    if half and j:
                        sp.wait_ge(scores_ready, GH * half0_blocks)
                    src = k_bands[half, :, :, T * j:T * (j + 1)].rearrange("b (d h) t -> (b d) h t", h=HALF)
                    sp.dma_start(keys[0:KR, kslot(half, j)], src).then_inc(k_loaded[kslot(half, j)], 16)
                elif kind == "query_load":
                    n = step[1]
                    stored_parts(sp, q_step[n])
                    if n >= QSLOTS:
                        sp.wait_ge(scores_ready, GH * (last_block[n - QSLOTS] + 1))
                    j, h0 = tile_of(n), GH * (n % 2)
                    src = q_bands[half_of(n), :, :, T * j:T * (j + 1)].rearrange("b (d h) t -> (b d) h t", h=HALF)
                    sp.dma_start(queries[0:KR, n % QSLOTS], src[:, h0:h0 + GH]).then_inc(q_loaded[n % QSLOTS], 16)
                elif kind == "value_store":
                    j = step[1]
                    sp.wait_ge(v_ready, 2 * (j + 1))
                    sp.dma_start(v_other[j], v_out[:].rearrange("p a v -> p (a v)")).then_inc(v_stored, 16)
                    if not late:
                        late = True
                        for name, src in (("wo", wo_t), ("wr", wr_t), ("wkf", wkf_t), ("wvf", wvf_t)):
                            load_w(name, src)
                        sp.dma_start(mu[:, 0], mu_k).then_inc(mu_loaded, 16)
                        sp.dma_start(mu[:, 1], mu_r).then_inc(mu_loaded, 16)
                elif kind == "value_load":
                    j = step[1]
                    sp.wait_ge(v_stored, 16 * NT)
                    sp.wait_ge(ones_ready, 3)
                    if j:
                        sp.wait_ge(values_done, half0_blocks)
                    s = kslot(1, j)
                    sp.dma_start(values[:, s].rearrange("p a v -> p (a v)"), v_other[j]).then_inc(v_loaded[s], 16)
                elif kind == "turn_max":
                    n = step[1]
                    sp.wait_ge(max_turned_ready, n + 1)
                    for r in range(3):
                        dst = queries[KR + r:KR + r + 1, n % QSLOTS].rearrange("o h (a q) -> o (h a) q", q=P)
                        sp.dma_start(dst, max_turned[GH * TB * r:GH * TB * (r + 1), n % 2])\
                            .then_inc(m_loaded[n % QSLOTS], 16)
                elif kind == "ctx_out":
                    n = step[1]
                    sp.wait_ge(ctx_ready, n + 1)
                    j, r0 = tile_of(n), P * (2 * half_of(n) + n % 2)
                    sp.dma_start(ctx_dram[r0:r0 + P, T * j:T * (j + 1)], ctx_sb[:, n % 2])\
                        .then_inc(ctx_stored[n % 2], 16)
                elif kind == "sums_load":
                    _, half, j = step
                    for g in range(2):
                        sp.wait_ge(ctx_stored[g], 16 * (NT * half + j + 1))
                    if number[step]:
                        sp.wait_ge(sums_stored, 16 * number[step])
                    src = ctx_dram[:, T * j:T * (j + 1)].rearrange("(f h r) (a t) -> f r h a t", f=2, r=32, a=HALF)
                    sp.dma_start(sums[:], src[half, DK]).then_inc(sums_loaded, 16)
                elif kind == "sums_store":
                    _, half, j = step
                    sp.wait_ge(sums_ready, number[step] + 1)
                    dst = recip_dram[half, :, T * j:T * (j + 1)].rearrange("h (a t) -> h a t", a=HALF)
                    sp.dma_start(dst, sums[:]).then_inc(sums_stored, 16)
                elif kind == "ctx_load":
                    j = step[1]
                    sp.wait_ge(sums_stored, 16 * (number["sums_store", 1, j] + 1))
                    if j:
                        sp.wait_ge(work_ready, unit_of["attn_out", j - 1, 1] + 1)
                        sp.wait_ge(ctx_normed, j)
                    src = ctx_dram[:, T * j:T * (j + 1)].rearrange("(c h r) t -> c h r t", c=NC, r=32)
                    for c in range(NC):
                        r = recip_dram[c, :, T * j:T * (j + 1)].unsqueeze(1).broadcast_to([HALF, DK, T])
                        sp.dma_start(recip_in[:, c], r)\
                            .then_inc(ctx_loaded, 16)
                        sp.dma_start(ctx_in[:, c], src[c, :, 0:DK]).then_inc(ctx_loaded, 16)
                elif kind == "out_store":
                    j = step[1]
                    sp.wait_ge(out_ready, 2 * (j + 1))
                    sp.dma_start(out_tiles[j], x2[:]).then_inc(out_stored, 16)
            sp.wait_ge(out_stored, 16 * NT)

        @block.gpsimd
        def _(pool):
            chain = [0]

            def link(ins):
                chain[0] += 1
                ins.then_inc(pool_chain, 1)
                pool.wait_ge(pool_chain, chain[0])

            nc.gpsimd.memset(ident[:], 0.0).then_inc(pool_chain, 1)
            nc.gpsimd.memset(ident_b[:], 0.0).then_inc(pool_chain, 1)
            nc.gpsimd.memset(mask[:], 0.0).then_inc(pool_chain, 1)
            nc.gpsimd.memset(minus_half[:], -0.5).then_inc(pool_chain, 1)
            chain[0] = 4
            pool.wait_ge(pool_chain, 4)
            for m in (ident, ident_b):
                nc.gpsimd.affine_select(out=m[:], in_=m[:], compare_op=ALU.not_equal, fill=1.0, base=0,
                                        pattern=[[-1, P]], channel_multiplier=1).then_inc(consts_ready, 1)
            diagonal = mask[:, T - P:T]
            nc.gpsimd.affine_select(out=diagonal, in_=diagonal, compare_op=ALU.is_ge, fill=NEG, base=0,
                                    pattern=[[-1, P]], channel_multiplier=1).then_inc(mask_made, 1)
            zero = nc.gpsimd.to_reg(0.0)
            nc.gpsimd.memset(v_out[:], 1.0).then_inc(ones_ready, 1)
            nc.gpsimd.memset(values[:], 1.0).then_inc(ones_ready, 1)
            nc.gpsimd.memset(x2T[:, :, 0:1], 0.0).then_inc(ones_ready, 1)
            for step in plan:
                kind = step[0]
                if kind == "mask":
                    _, n, kb, i = step
                    s = GH * block_of[n, kb] + i
                    pool.wait_ge(probs_ready, s + 1)
                    diagonal = probs[:, s % PSLOTS, 0:P]
                    nc.gpsimd.affine_select(out=diagonal, in_=diagonal, compare_op=ALU.is_ge, fill=zero, base=0,
                                            pattern=[[1, P]], channel_multiplier=-1).then_inc(probs_masked, 1)
                elif kind == "ln":
                    l = step[1]
                    pool.wait_ge(ln_stats, l + 1)
                    if l >= 2:
                        pool.wait_ge(xn_ready, l - 1)
                    link(nc.gpsimd.tensor_tensor(norm[:, l % 2, 0], var_mean[:, 0], minus_half[:], ALU.pow))
                    nc.gpsimd.tensor_tensor(norm[:, l % 2, 1], var_mean[:, 1], norm[:, l % 2, 0], ALU.mult)\
                        .then_inc(norm_ready, 1)
                    for slot in ([l] if l < NT - 1 else [l, l + 1] if l == NT - 1 else []):
                        pool.wait_ge(norm_ready, l + 1)
                        nc.gpsimd.memset(keys[KR:KM, slot].rearrange("p h t -> p (h t)").bitcast(U32), 0x3F803F80)\
                            .then_inc(key_ones, 1)
                        pool.wait_ge(key_ones, slot + 1)
                elif kind in ("key", "query"):
                    i = number[step]
                    pool.wait_ge(rest_ready, i + 1)
                    link(nc.gpsimd.tensor_scalar(parts[:, i % 2, 1], rest[:, i % 2], 1.0, 1.0, ALU.mult, ALU.mult))
                    nc.gpsimd.tensor_tensor(parts[:, i % 2, 2], rest[:, i % 2], parts[:, i % 2, 1],
                                            ALU.subtract).then_inc(parts_ready, 1)
                elif kind == "negmax":
                    n = step[1]
                    pool.wait_ge(neg_max_ready, n + 1)
                    if n >= 2:
                        pool.wait_ge(work_ready, unit_of["turn_max", n - 2] + 1)
                    m, mp = neg_max[:, n % 2], max_parts[:, n % 2]
                    link(nc.gpsimd.tensor_scalar(mp[:, 0], m, 1.0, 1.0, ALU.mult, ALU.mult))
                    link(nc.gpsimd.tensor_tensor(max_rest[:], m, mp[:, 0], ALU.subtract))
                    link(nc.gpsimd.tensor_scalar(mp[:, 1], max_rest[:], 1.0, 1.0, ALU.mult, ALU.mult))
                    nc.gpsimd.tensor_tensor(mp[:, 2], max_rest[:], mp[:, 1], ALU.subtract)\
                        .then_inc(max_parts_ready, 1)
                elif kind == "attn_norm":
                    pool.wait_ge(ctx_loaded, 16 * 2 * NC * (step[1] + 1))
                    nc.gpsimd.tensor_tensor(ctx_in[:], ctx_in[:], recip_in[:], ALU.mult).then_inc(ctx_normed, 1)
                elif kind == "mix":
                    j = step[1]
                    pool.wait_ge(xT_ready, NC * (NT + j + 1))
                    if j == 0:
                        pool.wait_ge(one_minus_ready, 1)
                        pool.wait_ge(ones_ready, 3)
                        pool.wait_ge(work_ready, last_prologue_unit[NT - 1] + 1)
                    else:
                        pool.wait_ge(work_ready, unit_of["gate", j - 1, 1] + 1)
                    for a, m in enumerate((mixk, mixr)):
                        for c in range(NC):
                            nc.gpsimd.tensor_scalar(m[:, c], x2T[:, c, 0:T], one_minus_mu[:, a, c:c + 1], 1.0,
                                                    ALU.mult, ALU.mult).then_inc(mix_prev, 1)
                elif kind == "up":
                    oc = step[2]
                    pool.wait_ge(relu_ready, number[step] + 1)
                    nc.gpsimd.tensor_tensor(hidden[:, oc], hidden[:, oc], hidden[:, oc], ALU.mult)\
                        .then_inc(hidden_ready, 1)
                elif kind == "gate":
                    i2 = step[2]
                    pool.wait_ge(tanh_ready, number[step] + 1)
                    nc.gpsimd.tensor_scalar(gate[:, i2], gate[:, i2], 0.5, 0.5, ALU.mult, ALU.add)\
                        .then_inc(gate_ready, 1)
                elif kind == "down":
                    i2 = step[2]
                    pool.wait_ge(y_ready, number[step] + 1)
                    xo = x2[:, 2 * i2:2 * i2 + 2].rearrange("p a c -> p (a c)")
                    nc.gpsimd.tensor_tensor(xo, xo, gate[:, i2], ALU.add).then_inc(out_ready, 1)

        @block.scalar
        def _(act):
            for step in plan:
                kind = step[0]
                u = unit_of.get(step)
                if kind == "score":
                    _, n, kb, i = step
                    s = GH * block_of[n, kb] + i
                    cols = T - P * max(0, kb - TB * tile_of(n))
                    act.wait_ge(scores_ready, s + 1)
                    if s >= PSLOTS:
                        act.wait_ge(values_done, (s - PSLOTS) // GH + 1)
                    nc.scalar.activation(probs[:, s % PSLOTS, 0:cols], scores[:, s % SRING, 0:cols], ACT.Exp)\
                        .then_inc(probs_ready, 1)
                elif kind == "ctx_out":
                    n = step[1]
                    act.wait_ge(values_done, last_block[n] + 1)
                    if n >= 2:
                        act.wait_ge(ctx_stored[n % 2], 16 * (n // 2))
                    nc.scalar.copy(ctx_sb[:, n % 2], ctx_ps[:, n % CBANKS]).then_inc(ctx_ready, 1)
                elif kind == "normalize":
                    l = step[1]
                    act.wait_ge(norm_ready, l + 1)
                    if l:
                        act.wait_ge(work_ready, unit_of["turn", l - 1, NC - 1] + 1)
                    src = x_in[:, l % 2] if l < NT else x2
                    for i in range(TB):
                        last = nc.scalar.activation(xn[:, i], src[:, i], ACT.Identity,
                                                    bias=norm[:, l % 2, 1, i:i + 1], scale=norm[:, l % 2, 0, i:i + 1])
                    last.then_inc(xn_ready, 1)
                elif kind == "turn":
                    _, l, c = step
                    if l < NT:
                        if l:
                            act.wait_ge(work_ready, last_prologue_unit[l - 1] + 1)
                        dst = xnT[:, c]
                    else:
                        if l > NT:
                            act.wait_ge(mix_ready, 4 * (l - NT))
                            act.wait_ge(xT_ready, NC * l)
                            nc.scalar.copy(x2T[:, c, 0:1], x2T[:, c, T:T + 1]).then_inc(last_token_kept, 1)
                            act.wait_ge(last_token_kept, NC * (l - NT - 1) + c + 1)
                        dst = x2T[:, c, 1:T + 1]
                    act.wait_ge(work_ready, u + 1)
                    nc.scalar.copy(dst, work[:, u % RING]).then_inc(xT_ready, 1)
                elif kind in ("key", "query"):
                    i = number[step]
                    act.wait_ge(work_ready, u + 1)
                    if i >= 2:
                        act.wait_ge(parts_stored[i % 2], 16 * len(RUNS) * (i // 2))
                    nc.scalar.mul(parts[:, i % 2, 0], work[:, u % RING], 1.0 if kind == "key" else DK ** -0.5)\
                        .then_inc(high_ready, 1)
                elif kind == "value":
                    _, j, i2 = step
                    act.wait_ge(work_ready, u + 1)
                    act.wait_ge(ones_ready, 2)
                    if j:
                        act.wait_ge(v_stored, 16 * j)
                    src = work[:, u % RING].rearrange("p (a f h d) -> p a f h d", a=2, f=2, d=DK)
                    for f, dst in enumerate((values[:, j], v_out)):
                        d4 = dst[:, 2 * i2:2 * i2 + 2, 0:HALF * VW].rearrange("p a (h v) -> p a h v", v=VW)
                        for a in range(2):
                            last = nc.scalar.copy(d4[:, a, :, 0:DK], src[:, a, f])
                    last.then_inc(v_ready, 1)
                elif kind == "turn_max":
                    n = step[1]
                    act.wait_ge(work_ready, u + 1)
                    if n >= 2:
                        act.wait_ge(m_loaded[(n - 2) % QSLOTS], 48 * ((n - 2) // QSLOTS + 1))
                    nc.scalar.copy(max_turned[:, n % 2], work[0:3 * GH * TB, u % RING].bitcast(BF16)[:, 0:P])\
                        .then_inc(max_turned_ready, 1)
                elif kind == "up":
                    _, j, oc = step
                    act.wait_ge(work_ready, u + 1)
                    if j:
                        act.wait_ge(work_ready, unit_of["down", j - 1, 1] + 1)
                    nc.scalar.activation(hidden[:, oc], work[:, u % RING], ACT.Relu).then_inc(relu_ready, 1)
                elif kind == "gate":
                    _, j, i2 = step
                    act.wait_ge(work_ready, u + 1)
                    if j:
                        act.wait_ge(out_ready, 2 * j)
                    nc.scalar.activation(gate[:, i2], work[:, u % RING], ACT.Tanh, scale=0.5)\
                        .then_inc(tanh_ready, 1)

        @block.vector
        def _(dve):
            chain = [0]

            def link(ins):
                chain[0] += 1
                ins.then_inc(dve_chain, 1)
                dve.wait_ge(dve_chain, chain[0])

            first_ln2 = True
            for step in after_next_max(plan, ("key", "query", "attn_out", "down")):
                kind = step[0]
                u = unit_of.get(step)
                if kind == "max":
                    _, n, i, qt, p = step
                    cols = T if p < tile_of(n) else P * (qt + 1)
                    dve.wait_ge(work_ready, u + 1)
                    bank, row = work[:, u % RING, 0:cols], row_max[:, n % 2, TB * i + qt, p:p + 1]
                    if p < tile_of(n):
                        nc.vector.reduce_max(row, bank, AXX).then_inc(max_done, 1)
                    else:
                        if n == 0:
                            dve.wait_ge(mask_made, 1)
                        nc.vector.tensor_tensor_reduce(bank, bank, mask[:, T - cols:T], 1.0, LOWEST,
                                                       ALU.add, ALU.max, row).then_inc(max_done, 1)
                elif kind == "negmax":
                    n = step[1]
                    dve.wait_ge(max_done, max_through[n])
                    if n >= 2:
                        dve.wait_ge(max_parts_ready, n - 1)
                    nc.vector.tensor_reduce(neg_max[:, n % 2], row_max[:, n % 2, :, 0:tile_of(n) + 1], AXX, ALU.max,
                                            negate=True).then_inc(neg_max_ready, 1)
                elif kind == "ln":
                    l = step[1]
                    if l < NT:
                        dve.wait_ge(x_loaded[l % 2], 16 * (l // 2 + 1))
                    else:
                        dve.wait_ge(x2_ready, 2 * (l - NT + 1))
                    if l:
                        dve.wait_ge(norm_ready, l)
                    src = x_in[:, l % 2] if l < NT else x2
                    for i in range(TB):
                        last = nc.vector.bn_stats(bn[:, i], src[:, i])
                    link(last)
                    for i in range(TB):
                        last = nc.vector.bn_aggr(mean_var[:, i], bn[:, i])
                    link(last)
                    nc.vector.tensor_scalar(var_mean[:, 0], mean_var[:, :, 1], EPS, None, ALU.add)
                    nc.vector.tensor_scalar(var_mean[:, 1], mean_var[:, :, 0], -1.0, None, ALU.mult)\
                        .then_inc(ln_stats, 1)
                elif kind in ("key", "query"):
                    i = number[step]
                    dve.wait_ge(high_ready, i + 1)
                    if i >= 2:
                        dve.wait_ge(parts_ready, i - 1)
                    nc.vector.scalar_tensor_tensor(out=rest[:, i % 2], in0=work[:, u % RING],
                                                   scalar=1.0 if kind == "key" else DK ** -0.5,
                                                   in1=parts[:, i % 2, 0], op0=ALU.mult, op1=ALU.subtract)\
                        .then_inc(rest_ready, 1)
                elif kind == "sums":
                    dve.wait_ge(sums_loaded, 16 * (number[step] + 1))
                    nc.vector.reciprocal(sums[:], sums[:]).then_inc(sums_ready, 1)
                elif kind == "attn_out":
                    _, j, i2 = step
                    dve.wait_ge(work_ready, u + 1)
                    dve.wait_ge(x_loaded[j % 2], 16 * ((NT + j) // 2 + 1))
                    if j:
                        dve.wait_ge(out_stored, 16 * j)
                    nc.vector.tensor_tensor(x2[:, 2 * i2:2 * i2 + 2],
                                            work[:, u % RING].rearrange("p (a c) -> p a c", a=2),
                                            x_in[:, j % 2, 2 * i2:2 * i2 + 2], ALU.add).then_inc(x2_ready, 1)
                elif kind == "mix":
                    j = step[1]
                    if first_ln2:
                        first_ln2 = False
                        dve.wait_ge(mu_loaded, 32)
                        nc.vector.tensor_scalar(one_minus_mu[:], mu[:], -1.0, 1.0, ALU.mult, ALU.add)\
                            .then_inc(one_minus_ready, 1)
                    for a, m in enumerate((mixk, mixr)):
                        for c in range(NC):
                            dve.wait_ge(mix_prev, 4 * j + 2 * a + c + 1)
                            nc.vector.scalar_tensor_tensor(out=m[:, c], in0=x2T[:, c, 1:T + 1],
                                                           scalar=mu[:, a, c:c + 1], in1=m[:, c],
                                                           op0=ALU.mult, op1=ALU.add).then_inc(mix_ready, 1)
                elif kind == "down":
                    i2 = step[2]
                    dve.wait_ge(work_ready, u + 1)
                    dve.wait_ge(gate_ready, number[step] + 1)
                    nc.vector.tensor_tensor(gate[:, i2], work[:, u % RING], gate[:, i2], ALU.mult)\
                        .then_inc(y_ready, 1)

        @block.tensor
        def _(pe):
            def own_bank(u):
                if u >= RING:
                    before = units[u - RING]
                    pe.wait_ge(released_by[before[0]], number[before] + 1)
                return work[:, u % RING]

            pe.wait_ge(consts_ready, 2)
            for step in plan:
                kind = step[0]
                u = unit_of.get(step)
                if kind == "score":
                    _, n, kb, i = step
                    j, half = tile_of(n), half_of(n)
                    off = P * max(0, kb - TB * j)
                    slot = kslot(half, kb // TB)
                    s = GH * block_of[n, kb] + i
                    if kb == 0 and i == 0:
                        pe.wait_ge(m_loaded[n % QSLOTS], 48 * (n // QSLOTS + 1))
                    if kb % TB == 0 and i == 0:
                        pe.wait_ge(key_ones, slot + 1)
                        pe.wait_ge(k_loaded[slot], 16 * slot_loads(half, kb // TB))
                    if s >= SRING:
                        pe.wait_ge(probs_ready, s - SRING + 1)
                    last = nc.tensor.matmul(scores[:, s % SRING, 0:T - off],
                                            keys[0:KM, slot, GH * (n % 2) + i, P * (kb % TB):P * (kb % TB + 1)],
                                            queries[0:KM, n % QSLOTS, i, off:T], start=True, stop=True)
                    last.then_inc(scores_ready, 1)
                elif kind == "probs_values":
                    _, n, kb = step
                    off = P * max(0, kb - TB * tile_of(n))
                    g = block_of[n, kb]
                    half, c = half_of(n), kb // TB
                    pe.wait_ge(probs_ready, GH * (g + 1))
                    if kb >= TB * tile_of(n):
                        pe.wait_ge(probs_masked, number["mask", n, kb, GH - 1] + 1)
                    if kb == 0 and n >= CBANKS:
                        pe.wait_ge(ctx_ready, n - CBANKS + 1)
                    if half == 0 and kb % TB == 0:
                        pe.wait_ge(v_ready, 2 * (c + 1))
                    elif half == 1 and kb % TB == 0:
                        pe.wait_ge(v_loaded[kslot(1, c)], 16)
                    for i in range(GH):
                        v0 = VW * (GH * (n % 2) + i)
                        last = nc.tensor.matmul(ctx_ps[32 * i:32 * i + 32, n % CBANKS, off:T],
                                                values[:, kslot(half, c), kb % TB, v0:v0 + 32],
                                                probs[:, (GH * g + i) % PSLOTS, 0:T - off],
                                                start=(kb == 0), stop=(kb == TB * (tile_of(n) + 1) - 1),
                                                tile_position=(0, 32 * i))
                    last.then_inc(values_done, 1)
                elif kind == "max":
                    _, n, i, qt, p = step
                    half = half_of(n)
                    cols = T if p < tile_of(n) else P * (qt + 1)
                    if i == 0 and qt == 0:
                        if p == 0:
                            pe.wait_ge(q_loaded[n % QSLOTS], 16 * (n // QSLOTS + 1))
                        pe.wait_ge(k_loaded[kslot(half, p)], 16 * slot_loads(half, p))
                    bank = own_bank(u)
                    last = nc.tensor.matmul(bank[:, 0:cols], queries[0:KR, n % QSLOTS, i, P * qt:P * (qt + 1)],
                                            keys[0:KR, kslot(half, p), GH * (n % 2) + i, 0:cols],
                                            start=True, stop=True)
                    last.then_inc(work_ready, 1)
                elif kind == "turn_max":
                    n = step[1]
                    pe.wait_ge(max_parts_ready, n + 1)
                    bank = own_bank(u)
                    nc.tensor.transpose(bank[0:3 * GH * TB].bitcast(BF16)[:, 0:P],
                                        max_parts[:, n % 2].rearrange("p r m -> p (r m)"), ident_b[:])\
                        .then_inc(work_ready, 1)
                elif kind == "turn":
                    _, l, c = step
                    pe.wait_ge(xn_ready, l + 1)
                    bank = own_bank(u)
                    for i in range(TB):
                        last = nc.tensor.transpose(bank[:, P * i:P * (i + 1)], xn[:, i, P * c:P * (c + 1)], ident[:])
                    last.then_inc(work_ready, 1)
                elif kind in ("key", "query", "up"):
                    _, j, oc = step
                    if kind == "up":
                        pe.wait_ge(mix_ready, 4 * j + 2)
                    else:
                        pe.wait_ge(xT_ready, NC * (j + 1))
                    name = {"key": "wk", "query": "wq", "up": "wkf"}[kind]
                    if j == 0:
                        pe.wait_ge(w_loaded[name], 16)
                    rhs = mixk if kind == "up" else xnT
                    bank = own_bank(u)
                    for c in range(NC):
                        last = nc.tensor.matmul(bank, w[name][:, c, P * oc:P * (oc + 1)], rhs[:, c],
                                                start=(c == 0), stop=(c == NC - 1))
                    last.then_inc(work_ready, 1)
                elif kind in ("value", "attn_out", "gate", "down"):
                    _, j, i2 = step
                    if kind == "value":
                        pe.wait_ge(xT_ready, NC * (j + 1))
                    elif kind == "attn_out":
                        pe.wait_ge(ctx_normed, j + 1)
                    elif kind == "gate":
                        pe.wait_ge(mix_ready, 4 * (j + 1))
                    else:
                        pe.wait_ge(hidden_ready, 2 * (j + 1))
                    name, lhs = {"value": ("wv", xnT), "attn_out": ("wo", ctx_in), "gate": ("wr", mixr),
                                 "down": ("wvf", hidden)}[kind]
                    if j == 0:
                        pe.wait_ge(w_loaded[name], 16)
                    bank = own_bank(u)
                    for a in range(2):
                        t0 = P * (2 * i2 + a)
                        for c in range(NC):
                            last = nc.tensor.matmul(bank[:, D * a:D * (a + 1)], lhs[:, c, t0:t0 + P], w[name][:, c],
                                                    start=(c == 0), stop=(c == NC - 1))
                    last.then_inc(work_ready, 1)


def kernel(L0_attn_x, L0_attn_wq, L0_attn_wk, L0_attn_wv, L0_attn_wo, L0_ffn_W_r, L0_ffn_W_k, L0_ffn_W_v,
           L0_ffn_mu_r, L0_ffn_mu_k):
    import numpy as np
    import concourse.bacc as bacc
    from concourse.bass_utils import run_bass_kernel_spmd

    x = np.asarray(L0_attn_x)
    laid_out = {"x": x.reshape(x.shape[1], x.shape[2])}
    for name, weight in (("wq_t", L0_attn_wq), ("wk_t", L0_attn_wk), ("wv_t", L0_attn_wv), ("wo_t", L0_attn_wo),
                         ("wr_t", L0_ffn_W_r), ("wkf_t", L0_ffn_W_k), ("wvf_t", L0_ffn_W_v)):
        w_t = np.asarray(weight).T
        if name in ("wq_t", "wk_t"):
            w_t = w_t.reshape(D, 2, HALF, DK).transpose(0, 1, 3, 2).reshape(D, D)
        laid_out[name] = np.ascontiguousarray(w_t)
    for name, mix in (("mu_r", L0_ffn_mu_r), ("mu_k", L0_ffn_mu_k)):
        laid_out[name] = np.ascontiguousarray(np.asarray(mix).reshape(NC, P).T)
    nc = bacc.Bacc("TRN2", target_bir_lowering=False, num_devices=1)
    args = {name: nc.dram_tensor(name, a.shape, mybir.dt.from_np(a.dtype), kind="ExternalInput").ap()
            for name, a in laid_out.items()}
    out = nc.dram_tensor("out", (S, D), F32, kind="ExternalOutput").ap()
    attention_ffn(nc, out=out, **args)
    result = run_bass_kernel_spmd(nc, [laid_out], core_ids=[0])
    return result.results[0]["out"].reshape(x.shape)
```

```python
from contextlib import ExitStack

import concourse.bass as bass
from concourse import mybir

ALU = mybir.AluOpType
ACT = mybir.ActivationFunctionType
AXX = mybir.AxisListType.X
F32 = mybir.dt.float32
BF16 = mybir.dt.bfloat16
U32 = mybir.dt.uint32

P = 128
S, D, H = 4096, 256, 16
DK = D // H
T = 512
NT = S // T
TB = T // P
NC = D // P
HALF = H // 2
GH = 4
GROUPS = 2 * NT * 2
KSLOTS = NT + 1
QSLOTS = 5
PSLOTS = 8
RING = 3
SRING = 4
CBANKS = 1
VW = DK + 1
VB = HALF * VW
VS = TB * VB + 32 - DK
EPS = 1e-5
NEG = -1e30
LOWEST = -3e38
RUNS = ((0, (0, 1, 2), (0, 0, 0)), (3, (0, 1), (1, 1)), (5, (0,), (2,)))
BANDS = sum(len(parts) for _, parts, _ in RUNS)
KR = BANDS * DK
KM = KR + 3


def tile_of(n):
    return n % (2 * NT) // 2


def half_of(n):
    return n // (2 * NT)


def kslot(half, c):
    return (NT * half + c) % KSLOTS


WORK = ("max", "turn_max", "turn", "key", "query", "value", "attn_out", "up", "gate", "down")
HOLD = {
    "score": (("pe", 0.22), ("act", 0.48)), "mask": (("pool", 0.193),), "probs_values": (("pe", 0.807),),
    "max": (("pe", 0.22), ("dve", 0.60)), "negmax": (("dve", 0.282),), "max_parts": (("pool", 1.006),),
    "turn_max": (("pe", 0.07), ("act", 0.371)), "max_load": (("sp", 0.2), ("dma", 0.253)),
    "query_load": (("sp", 0.1), ("dma", 1.116)), "ctx_out": (("act", 0.723),),
    "ctx_store": (("sp", 0.1), ("dma", 0.671)), "sums_load": (("sp", 0.1), ("dma", 0.006)),
    "sums": (("dve", 0.518),), "sums_store": (("sp", 0.1), ("dma", 0.098)), "x_load": (("sp", 0.1), ("dma", 1.382)),
    "ln": (("dve", 2.902),), "ln_norm": (("pool", 3.311),), "normalize": (("act", 2.786),),
    "turn": (("pe", 0.86), ("act", 0.537)), "key": (("pe", 1.71), ("act", 0.172)),
    "query": (("pe", 1.71), ("act", 0.417)), "split": (("pool", 4.979),), "store": (("sp", 0.3), ("dma", 2.176)),
    "value": (("pe", 1.71), ("act", 1.536)), "value_store": (("sp", 0.4), ("dma", 0.703)),
    "key_load": (("sp", 0.1), ("dma", 2.858)), "value_load": (("sp", 0.1), ("dma", 1.017)),
    "ctx_load": (("sp", 0.1), ("dma", 0.452)), "recip_load": (("sp", 0.1), ("dma", 0.348)),
    "attn_norm": (("pool", 0.856),), "attn_out": (("pe", 1.271),), "residual": (("dve", 0.6),),
    "mix_old": (("pool", 0.79),), "mix": (("dve", 1.725),), "up": (("pe", 1.71), ("act", 0.691)),
    "square": (("pool", 1.123),), "gate": (("pe", 1.71), ("act", 0.638)), "halve": (("pool", 0.626),),
    "down": (("pe", 1.374),), "gated": (("dve", 0.743),), "output": (("pool", 1.843),),
    "out_store": (("sp", 0.1), ("dma", 1.524)),
}
HOP = 0.2
DMA = 2.29
EARLY = {"max": 0.3, "probs_values": -0.225, "score": 0.304}
OTHER_EVERY = 4.855
TURN_AFTER = 9
CHOICE = 0.28


def block_width(n, kb):
    return T - P * max(0, kb - TB * tile_of(n))


def hold(step):
    kind, share = step[0], 1.0
    if kind == "split" and step[1][1] == 0:
        return [("dve", 2.6)]
    if kind in ("score", "probs_values"):
        share = block_width(step[1], step[2]) / T
    elif kind == "max" and step[4] == tile_of(step[1]):
        share = (step[3] + 1) / TB
    return [(engine, us * share + (0.06 if share < 1.0 else 0.0)) for engine, us in HOLD[kind]]


def needs(step):
    kind, a = step[0], step[1]
    b = step[2] if len(step) > 2 else None
    if kind == "score":
        kb, j, half = b, tile_of(a), half_of(a)
        return [("max_load", a), ("key_load", half, kb // TB)]
    if kind == "mask":
        return [("score",) + step[1:]]
    if kind == "probs_values":
        half, c = half_of(a), b // TB
        return ([("mask" if b >= TB * tile_of(a) else "score", a, b, GH - 1)]
                + ([("ctx_out", a - CBANKS)] if b == 0 and a >= CBANKS else [])
                + ([("value", c, 1)] if half == 0 else [("value_load", c)]))
    if kind == "ctx_out":
        return [("probs_values", a, TB * (tile_of(a) + 1) - 1)] + ([("ctx_store", a - 2)] if a >= 2 else [])
    if kind == "ctx_store":
        return [("ctx_out", a)]
    if kind == "max":
        return [("query_load", a), ("key_load", half_of(a), step[4])]
    if kind == "negmax":
        return [("max", a, GH - 1, TB - 1, tile_of(a))] + ([("max_parts", a - 2)] if a >= 2 else [])
    if kind == "max_parts":
        return [("negmax", a)] + ([("turn_max", a - 2)] if a >= 2 else [])
    if kind == "turn_max":
        return [("max_parts", a)] + ([("max_load", a - 2)] if a >= 2 else [])
    if kind == "max_load":
        return [("turn_max", a)]
    if kind == "query_load":
        return ([("store", ("query", tile_of(a), half_of(a)))]
                + ([("score", a - QSLOTS, TB * (tile_of(a - QSLOTS) + 1) - 1, GH - 1)] if a >= QSLOTS else []))
    if kind == "key_load":
        return [("store", ("key", b, a))] + ([("score", 2 * NT - 1, TB * b - 1, GH - 1)] if a and b else [])
    if kind == "value_load":
        return [("value_store", NT - 1)] + ([("probs_values", 2 * NT - 1, TB * a - 1)] if a else [])
    if kind == "x_load":
        return ([] if a < 2 else [("normalize", a - 2)] if a < NT + 2 else [("residual", ("attn_out", a - 2 - NT, 1))])
    if kind == "ln":
        return ([("x_load", a)] if a < NT else [("residual", ("attn_out", a - NT, 1))]) \
            + ([("ln_norm", a - 1)] if a else [])
    if kind == "ln_norm":
        return [("ln", a)] + ([("normalize", a - 2)] if a >= 2 else [])
    if kind == "normalize":
        return [("ln_norm", a)] + ([("turn", a - 1, NC - 1)] if a else [])
    if kind == "turn":
        return ([("normalize", a)] + ([("turn", a, b - 1)] if b else [])
                + (products_of(a - 1) if 0 < a < NT else [])
                + ([("mix", a - NT - 1)] if a > NT else []))
    if kind in ("key", "query", "value"):
        before = ORDER_QK.index(step) if kind != "value" else 0
        return ([("turn", a, NC - 1)]
                + ([("split", ORDER_QK[before - 2])] if before >= 2 else [])
                + ([ORDER_QK[before - 1]] if before else [])
                + ([("value_store", a - 1)] if kind == "value" and a else [])
                + ([("value", a, 0)] if kind == "value" and b else []))
    if kind == "split":
        i = ORDER_QK.index(a)
        return [a] + ([("split", ORDER_QK[i - 1])] if i else []) + ([("store", ORDER_QK[i - 2])] if i >= 2 else [])
    if kind == "store":
        return [("split", a)] + ([("store", ORDER_QK[ORDER_QK.index(a) - 1])] if ORDER_QK.index(a) else [])
    if kind == "value_store":
        return [("value", a, 1)]
    if kind == "sums_load":
        before = NT * a + b - 1
        return [("ctx_store", 2 * NT * a + 2 * b), ("ctx_store", 2 * NT * a + 2 * b + 1)] \
            + ([("sums_store", before // NT, before % NT)] if before >= 0 else [])
    if kind in ("sums", "sums_store"):
        return [({"sums": "sums_load", "sums_store": "sums"}[kind], a, b)]
    if kind == "ctx_load":
        return ([("ctx_store", 2 * NT * b + 2 * a), ("ctx_store", 2 * NT * b + 2 * a + 1)]
                + ([("attn_out", a - 1, 1)] if a else []))
    if kind == "recip_load":
        return [("sums_store", b, a)] + ([("attn_norm", a - 1, b)] if a else [])
    if kind == "attn_norm":
        return ([("ctx_load", a, b), ("recip_load", a, b)]
                + ([("attn_norm", a, 0)] if b else [("attn_norm", a - 1, 1)] if a else []))
    if kind == "attn_out":
        return [("attn_norm", a, 1), ("x_load", NT + a)] + ([("out_store", a - 1)] if a else []) \
            + ([("attn_out", a, 0)] if b else [])
    if kind == "mix_old":
        return [("turn", NT + a, NC - 1), ("gate", a - 1, 1) if a else ("query", NT - 1, 1)]
    if kind == "mix":
        return [("mix_old", a)]
    if kind == "up":
        return [("mix", a)] + ([("down", a - 1, 1)] if a else []) + ([("up", a, 0)] if b else [])
    if kind == "gate":
        return [("up", a, 1)] + ([("out_store", a - 1)] if a else []) + ([("gate", a, 0)] if b else [])
    if kind == "down":
        return [("square", ("up", a, 1)), ("halve", ("gate", a, 1))] + ([("down", a, 0)] if b else [])
    if kind == "output":
        return [("gated", a)] + ([("output", ("down", a[1], 0))] if a[2] else [])
    if kind == "out_store":
        return [("output", ("down", a, 1))]
    return [a] + ([(kind, a[:2] + (0,))] if a[2] else [])


ORDER_QK = [(kind, j, oc) for j in range(NT) for oc in range(2) for kind in ("key", "query")]
RELEASED = {"attn_out": "residual", "down": "gated"}


def products_of(j):
    return [("query", j, 1), ("value", j, 1)]


def make_plan():
    attention = [("score", n, kb, i) for n in range(GROUPS) for kb in range(TB * (tile_of(n) + 1)) for i in range(GH)]
    contexts = [("probs_values", n, kb) for n in range(GROUPS) for kb in range(TB * (tile_of(n) + 1))]
    maxima = []
    for n in range(GROUPS):
        first = len(maxima)
        maxima += [("max", n, i, qt, p) for i in range(GH) for qt in range(TB) for p in range(tile_of(n) + 1)]
        if n:
            maxima.insert(first + TURN_AFTER, ("turn_max", n - 1))
    maxima.append(("turn_max", GROUPS - 1))
    before, after = [], []
    for j in range(NT):
        before += [("turn", j, 0), ("turn", j, 1), ("key", j, 0), ("query", j, 0), ("value", j, 0), ("value", j, 1),
                   ("key", j, 1), ("query", j, 1)]
        after += [("attn_out", j, 0), ("attn_out", j, 1), ("turn", NT + j, 0), ("turn", NT + j, 1),
                  ("up", j, 0), ("up", j, 1), ("gate", j, 0), ("gate", j, 1), ("down", j, 0), ("down", j, 1)]
    waiting = [("mask", n, kb, i) for n in range(GROUPS) for kb in range(TB * tile_of(n), TB * (tile_of(n) + 1))
               for i in range(GH)]
    for n in range(GROUPS):
        waiting += [(kind, n) for kind in ("negmax", "max_parts", "max_load", "query_load", "ctx_out", "ctx_store")]
    for l in range(2 * NT):
        waiting += [(kind, l) for kind in ("x_load", "ln", "ln_norm", "normalize")]
    for step in ORDER_QK:
        waiting += [(kind, step) for kind in ("split", "store")]
    for j in range(NT):
        waiting += [(kind, j) for kind in ("value_store", "value_load", "mix_old", "mix", "out_store")]
        for half in range(2):
            waiting += [(kind, half, j) for kind in ("key_load", "sums_load", "sums", "sums_store")]
            waiting += [(kind, j, half) for kind in ("ctx_load", "recip_load", "attn_norm")]
            waiting += [("residual", ("attn_out", j, half)), ("square", ("up", j, half)),
                        ("halve", ("gate", j, half)), ("gated", ("down", j, half)), ("output", ("down", j, half))]

    missing, then = {}, {}
    for step in waiting:
        missing[step] = len(needs(step))
        for need in needs(step):
            then.setdefault(need, []).append(step)
    free = dict.fromkeys(("pe", "act", "dve", "pool", "sp", "dma"), 0.0)
    done, plan, ready, units = {}, [], [], []

    def ready_at(step):
        return max([done[need] + HOP for need in needs(step)], default=0.0)

    for step in waiting:
        if not missing[step]:
            ready.append((0.0, step))

    def place(step, t):
        for engine, us in hold(step):
            if step[0] == "score" and engine == "act":
                g = blocks[step[1:3]]
                if g >= 2:
                    t = max(t, done[contexts[g - 2]] + HOP)
            free[engine] = t = max(t, free[engine]) + us
            t += HOP
        t -= HOP
        if hold(step)[-1][0] == "dma":
            t += DMA
        done[step] = t
        plan.append(step)
        if step[0] in WORK:
            units.append(step)
        for follower in then.get(step, []):
            missing[follower] -= 1
            if not missing[follower]:
                ready.append((ready_at(follower), follower))

    blocks = {step[1:]: g for g, step in enumerate(contexts)}
    streams = {"score": attention, "probs_values": contexts, "max": maxima, "before": before, "after": after}
    at = dict.fromkeys(streams, 0)
    last_other = 0.0
    while any(at[name] < len(stream) for name, stream in streams.items()):
        while ready and min(ready)[0] <= free["pe"]:
            first = min(ready)
            ready.remove(first)
            place(first[1], first[0])
        best = None
        for name, stream in streams.items():
            if at[name] == len(stream):
                continue
            step = stream[at[name]]
            if any(need not in done for need in needs(step)):
                continue
            t = max(free["pe"], ready_at(step))
            if name == "score":
                s = at[name]
                if s >= SRING:
                    t = max(t, done[attention[s - SRING]] + HOP)
                if blocks[step[1:3]] >= 2 and at["probs_values"] < blocks[step[1:3]] - 1:
                    continue
                early = EARLY["score"]
            elif name == "probs_values":
                early = EARLY["probs_values"]
            else:
                if len(units) >= RING:
                    released = units[-RING]
                    released = (RELEASED[released[0]], released) if released[0] in RELEASED else released
                    if released not in done:
                        continue
                    t = max(t, done[released] + HOP)
                if name == "max":
                    ahead = step[1] - attention[min(at["score"], len(attention) - 1)][1]
                    early = EARLY["max"] + 0.1 * (3 - ahead)
                else:
                    every = OTHER_EVERY * (step[1] % NT + 1) / NT
                    early = min(0.797, (free["pe"] - last_other) - every)
            key = (t - CHOICE * early, -early)
            if best is None or key < best[0]:
                best = (key, t, name, step)
        if best is None or (ready and min(ready)[0] < best[1] and best[1] > free["pe"]):
            first = min(ready)
            ready.remove(first)
            place(first[1], first[0])
            continue
        _, t, name, step = best
        place(step, t)
        at[name] += 1
        if name in ("before", "after"):
            last_other = free["pe"]
    while ready:
        first = min(ready)
        ready.remove(first)
        place(first[1], first[0])
    return plan


def attention_ffn(nc, x, wq_t, wk_t, wv_t, wo_t, wr_t, wkf_t, wvf_t, mu_r, mu_k, out):
    plan = make_plan()

    number, count, unit_of, units = {}, {}, {}, []
    for step in plan:
        kind = "qk" if step[0] in ("key", "query") else step[0]
        number[step] = count.get(kind, 0)
        count[kind] = number[step] + 1
        if step[0] in WORK:
            unit_of[step] = len(units)
            units.append(step)
    block_of, n_blocks = {}, 0
    for n in range(GROUPS):
        for kb in range(TB * (tile_of(n) + 1)):
            block_of[n, kb] = n_blocks
            n_blocks += 1
    last_block = {n: block_of[n, TB * (tile_of(n) + 1) - 1] for n in range(GROUPS)}
    max_through = {}
    for step in units:
        if step[0] == "max":
            max_through[step[1]] = number[step] + 1

    def dram(name, shape, dt):
        return nc.dram_tensor(name, shape, dt, kind="Internal").ap()

    q_bands = dram("q_bands", [2, BANDS, P, S], BF16)
    k_bands = dram("k_bands", [2, BANDS, P, S], BF16)
    v_other = dram("v_other", [NT, P, VS], F32)
    ctx_dram = dram("ctx_dram", [32 * H, S], F32)
    recip_dram = dram("recip_dram", [2, HALF, S], F32)

    with ExitStack() as ctx:
        def sb(name, shape, dt=F32):
            return ctx.enter_context(nc.sbuf_tensor(name, shape, dt))

        def psum(name, shape):
            return ctx.enter_context(nc.psum_tensor(name, shape, F32))

        def sem(name):
            return ctx.enter_context(nc.semaphore(name))

        keys = sb("keys", [P, KSLOTS, HALF, T], BF16)
        queries = sb("queries", [P, QSLOTS, GH, T], BF16)
        values = sb("values", [P, KSLOTS, VS])
        probs = sb("probs", [P, PSLOTS, T])
        w = {name: sb(name, [P, NC, D]) for name in ("wq", "wk", "wv", "wo", "wr", "wkf", "wvf")}
        mu = sb("mu", [P, 2, NC])
        one_minus_mu = sb("one_minus_mu", [P, 2, NC])
        x_in = sb("x_in", [P, 2, TB, D])
        xn = sb("xn", [P, TB, D])
        xnT = sb("xnT", [P, NC, T])
        parts = sb("parts", [P, 2, 3, T], BF16)
        rest = sb("rest", [P, 2, T])
        v_out = sb("v_out", [P, VS])
        bn = sb("bn", [P, TB, 6])
        mean_var = sb("mean_var", [P, TB, 2])
        var_mean = sb("var_mean", [P, 2, TB])
        minus_half = sb("minus_half", [P, TB])
        norm = sb("norm", [P, 2, 2, TB])
        row_max = sb("row_max", [P, 2, GH * TB, NT])
        neg_max = sb("neg_max", [P, 2, GH * TB])
        max_rest = sb("max_rest", [P, GH * TB])
        max_parts = sb("max_parts", [P, 2, 3, GH * TB], BF16)
        max_turned = sb("max_turned", [3 * GH * TB, 2, P], BF16)
        ctx_sb = sb("ctx_sb", [P, 2, T])
        ctx_in = sb("ctx_in", [P, NC, T])
        recip_in = sb("recip_in", [P, NC, T])
        sums = sb("sums", [HALF * HALF, T // HALF])
        x2 = sb("x2", [P, TB, D])
        x2T = sb("x2T", [P, NC, T + 1])
        mixk = sb("mixk", [P, NC, T])
        mixr = xnT
        hidden = sb("hidden", [P, NC, T])
        gate = sb("gate", [P, 2, T])
        ident = sb("ident", [P, P])
        ident_b = sb("ident_b", [P, P], BF16)
        mask = sb("mask", [P, T], BF16)

        scores = psum("scores", [P, SRING, T])
        work = psum("work", [P, RING, T])
        ctx_ps = psum("ctx_ps", [P, CBANKS, T])

        consts_ready = sem("consts_ready")
        mask_made = sem("mask_made")
        ones_ready = sem("ones_ready")
        key_ones = sem("key_ones")
        one_minus_ready = sem("one_minus_ready")
        w_loaded = {name: sem(f"{name}_loaded") for name in w}
        mu_loaded = sem("mu_loaded")
        x_loaded = [sem(f"x_loaded{i}") for i in range(2)]
        ln_stats = sem("ln_stats")
        norm_ready = sem("norm_ready")
        xn_ready = sem("xn_ready")
        xT_ready = sem("xT_ready")
        product_kept = sem("product_kept")
        parts_ready = sem("parts_ready")
        parts_stored = [sem(f"parts_stored{i}") for i in range(2)]
        v_ready = sem("v_ready")
        v_stored = sem("v_stored")
        k_loaded = [sem(f"k_loaded{i}") for i in range(KSLOTS)]
        v_loaded = [sem(f"v_loaded{i}") for i in range(KSLOTS)]
        q_loaded = [sem(f"q_loaded{i}") for i in range(QSLOTS)]
        m_loaded = [sem(f"m_loaded{i}") for i in range(QSLOTS)]
        max_done = sem("max_done")
        neg_max_ready = sem("neg_max_ready")
        max_parts_ready = sem("max_parts_ready")
        max_turned_ready = sem("max_turned_ready")
        scores_ready = sem("scores_ready")
        work_ready = sem("work_ready")
        probs_ready = sem("probs_ready")
        probs_masked = sem("probs_masked")
        values_done = sem("values_done")
        ctx_ready = sem("ctx_ready")
        ctx_stored = [sem(f"ctx_stored{i}") for i in range(2)]
        sums_loaded = sem("sums_loaded")
        sums_ready = sem("sums_ready")
        sums_stored = sem("sums_stored")
        ctx_loaded = [sem(f"ctx_loaded{c}") for c in range(NC)]
        ctx_normed = sem("ctx_normed")
        x2_ready = sem("x2_ready")
        mix_prev = sem("mix_prev")
        mix_ready = sem("mix_ready")
        last_token_kept = sem("last_token_kept")
        relu_ready = sem("relu_ready")
        hidden_ready = sem("hidden_ready")
        tanh_ready = sem("tanh_ready")
        gate_ready = sem("gate_ready")
        y_ready = sem("y_ready")
        out_ready = sem("out_ready")
        out_stored = sem("out_stored")
        dve_chain = sem("dve_chain")
        pool_chain = sem("pool_chain")

        released_by = {"max": max_done, "turn_max": max_turned_ready, "turn": xT_ready,
                       "key": product_kept, "query": product_kept, "value": v_ready,
                       "attn_out": x2_ready, "up": relu_ready, "gate": tanh_ready, "down": y_ready}
        last_prologue_unit = {j: max(unit_of[s] for s in units if s[0] in ("key", "query", "value") and s[1] == j)
                              for j in range(NT)}
        q_step = {n: ("query", tile_of(n), half_of(n)) for n in range(GROUPS)}

        def stored_parts(eng, step):
            i = number[step]
            eng.wait_ge(parts_stored[i % 2], 16 * len(RUNS) * (i // 2 + 1))

        def split_product(eng, compute, link, i):
            eng.wait_ge(product_kept, i + 1)
            if i:
                eng.wait_ge(parts_ready, i)
            if i >= 2:
                eng.wait_ge(parts_stored[i % 2], 16 * len(RUNS) * (i // 2))
            left, part = rest[:, i % 2], parts[:, i % 2]
            link(compute.tensor_scalar(part[:, 0], left, 1.0, 1.0, ALU.mult, ALU.mult))
            link(compute.tensor_tensor(left, left, part[:, 0], ALU.subtract))
            link(compute.tensor_scalar(part[:, 1], left, 1.0, 1.0, ALU.mult, ALU.mult))
            compute.tensor_tensor(part[:, 2], left, part[:, 1], ALU.subtract).then_inc(parts_ready, 1)

        def slot_loads(half, c):
            return sum(kslot(a, b) == kslot(half, c) for a in range(half + 1) for b in range(NT)
                       if (a, b) <= (half, c))

        block = ctx.enter_context(nc.Block())

        @block.sync
        def _(sp):
            x_tiles = x.rearrange("(j i p) c -> j p i c", p=P, i=TB)
            out_tiles = out.rearrange("(j i p) c -> j p i c", p=P, i=TB)

            def load_w(name, src):
                sp.dma_start(w[name][:], src.rearrange("(c p) o -> p c o", p=P)).then_inc(w_loaded[name], 16)

            late = False
            for step in plan:
                kind = step[0]
                if kind == "x_load":
                    k = step[1]
                    if 2 <= k < NT + 2:
                        sp.wait_ge(xn_ready, TB * (k - 1))
                    elif k >= 2:
                        sp.wait_ge(x2_ready, 2 * (k - 1 - NT))
                    sp.dma_start(x_in[:, k % 2], x_tiles[k % NT]).then_inc(x_loaded[k % 2], 16)
                    if k == 0:
                        load_w("wk", wk_t)
                        load_w("wq", wq_t)
                        load_w("wv", wv_t)
                elif kind == "store":
                    kind, j, oc = step[1]
                    i = number[step[1]]
                    sp.wait_ge(parts_ready, i + 1)
                    for b, of_query, of_key in RUNS:
                        m = len(of_query)
                        if kind == "key":
                            src = parts[:, i % 2, of_key[0]:of_key[0] + 1].broadcast_to([P, m, T])
                        else:
                            src = parts[:, i % 2, 0:m]
                        dst = (k_bands if kind == "key" else q_bands)[oc, b:b + m, :, T * j:T * (j + 1)]
                        sp.dma_start(dst.rearrange("r p t -> p r t"), src).then_inc(parts_stored[i % 2], 16)
                elif kind == "key_load":
                    _, half, j = step
                    stored_parts(sp, ("key", j, half))
                    if half and j:
                        sp.wait_ge(scores_ready, GH * (block_of[2 * NT - 1, TB * j - 1] + 1))
                    src = k_bands[half, :, :, T * j:T * (j + 1)].rearrange("b (d h) t -> (b d) h t", h=HALF)
                    sp.dma_start(keys[0:KR, kslot(half, j)], src).then_inc(k_loaded[kslot(half, j)], 16)
                elif kind == "query_load":
                    n = step[1]
                    stored_parts(sp, q_step[n])
                    if n >= QSLOTS:
                        sp.wait_ge(scores_ready, GH * (last_block[n - QSLOTS] + 1))
                    j, h0 = tile_of(n), GH * (n % 2)
                    src = q_bands[half_of(n), :, :, T * j:T * (j + 1)].rearrange("b (d h) t -> (b d) h t", h=HALF)
                    sp.dma_start(queries[0:KR, n % QSLOTS], src[:, h0:h0 + GH]).then_inc(q_loaded[n % QSLOTS], 16)
                elif kind == "value_store":
                    j = step[1]
                    sp.wait_ge(v_ready, 2 * (j + 1))
                    sp.dma_start(v_other[j], v_out[:]).then_inc(v_stored, 16)
                    if not late:
                        late = True
                        for name, src in (("wo", wo_t), ("wr", wr_t), ("wkf", wkf_t), ("wvf", wvf_t)):
                            load_w(name, src)
                        sp.dma_start(mu[:, 0], mu_k).then_inc(mu_loaded, 16)
                        sp.dma_start(mu[:, 1], mu_r).then_inc(mu_loaded, 16)
                elif kind == "value_load":
                    j = step[1]
                    sp.wait_ge(v_stored, 16 * NT)
                    sp.wait_ge(ones_ready, 3)
                    if j:
                        sp.wait_ge(values_done, block_of[2 * NT - 1, TB * j - 1] + 1)
                    s = kslot(1, j)
                    sp.dma_start(values[:, s], v_other[j]).then_inc(v_loaded[s], 16)
                elif kind == "max_load":
                    n = step[1]
                    sp.wait_ge(max_turned_ready, n + 1)
                    for r in range(3):
                        dst = queries[KR + r:KR + r + 1, n % QSLOTS].rearrange("o h (a q) -> o (h a) q", q=P)
                        sp.dma_start(dst, max_turned[GH * TB * r:GH * TB * (r + 1), n % 2])\
                            .then_inc(m_loaded[n % QSLOTS], 16)
                elif kind == "ctx_store":
                    n = step[1]
                    sp.wait_ge(ctx_ready, n + 1)
                    j, r0 = tile_of(n), P * (2 * half_of(n) + n % 2)
                    sp.dma_start(ctx_dram[r0:r0 + P, T * j:T * (j + 1)], ctx_sb[:, n % 2])\
                        .then_inc(ctx_stored[n % 2], 16)
                elif kind == "sums_load":
                    _, half, j = step
                    for g in range(2):
                        sp.wait_ge(ctx_stored[g], 16 * (NT * half + j + 1))
                    if number[step]:
                        sp.wait_ge(sums_stored, 16 * number[step])
                    src = ctx_dram[:, T * j:T * (j + 1)].rearrange("(f h r) (a t) -> f r h a t", f=2, r=32, a=HALF)
                    sp.dma_start(sums[:], src[half, DK]).then_inc(sums_loaded, 16)
                elif kind == "sums_store":
                    _, half, j = step
                    sp.wait_ge(sums_ready, number[step] + 1)
                    dst = recip_dram[half, :, T * j:T * (j + 1)].rearrange("h (a t) -> h a t", a=HALF)
                    sp.dma_start(dst, sums[:]).then_inc(sums_stored, 16)
                elif kind == "ctx_load":
                    _, j, c = step
                    for g in range(2):
                        sp.wait_ge(ctx_stored[g], 16 * (NT * c + j + 1))
                    if j:
                        sp.wait_ge(work_ready, unit_of["attn_out", j - 1, 1] + 1)
                    src = ctx_dram[:, T * j:T * (j + 1)].rearrange("(c h r) t -> c h r t", c=NC, r=32)
                    sp.dma_start(ctx_in[:, c], src[c, :, 0:DK]).then_inc(ctx_loaded[c], 16)
                elif kind == "recip_load":
                    _, j, c = step
                    sp.wait_ge(sums_stored, 16 * (number["sums_store", c, j] + 1))
                    if j:
                        sp.wait_ge(ctx_normed, NC * (j - 1) + c + 1)
                    src = recip_dram[c, :, T * j:T * (j + 1)].unsqueeze(1).broadcast_to([HALF, DK, T])
                    sp.dma_start(recip_in[:, c], src).then_inc(ctx_loaded[c], 16)
                elif kind == "out_store":
                    j = step[1]
                    sp.wait_ge(out_ready, 2 * (j + 1))
                    sp.dma_start(out_tiles[j], x2[:]).then_inc(out_stored, 16)
            sp.wait_ge(out_stored, 16 * NT)

        @block.gpsimd
        def _(pool):
            chain = [0]

            def link(ins):
                chain[0] += 1
                ins.then_inc(pool_chain, 1)
                pool.wait_ge(pool_chain, chain[0])

            nc.gpsimd.memset(ident[:], 0.0).then_inc(pool_chain, 1)
            nc.gpsimd.memset(ident_b[:], 0.0).then_inc(pool_chain, 1)
            nc.gpsimd.memset(mask[:], 0.0).then_inc(pool_chain, 1)
            nc.gpsimd.memset(minus_half[:], -0.5).then_inc(pool_chain, 1)
            chain[0] = 4
            pool.wait_ge(pool_chain, 4)
            for m in (ident, ident_b):
                nc.gpsimd.affine_select(out=m[:], in_=m[:], compare_op=ALU.not_equal, fill=1.0, base=0,
                                        pattern=[[-1, P]], channel_multiplier=1).then_inc(consts_ready, 1)
            diagonal = mask[:, T - P:T]
            nc.gpsimd.affine_select(out=diagonal, in_=diagonal, compare_op=ALU.is_ge, fill=NEG, base=0,
                                    pattern=[[-1, P]], channel_multiplier=1).then_inc(mask_made, 1)
            zero = nc.gpsimd.to_reg(0.0)
            nc.gpsimd.memset(v_out[:], 1.0).then_inc(ones_ready, 1)
            nc.gpsimd.memset(x2T[:, :, 0:1], 0.0).then_inc(ones_ready, 1)
            for step in plan:
                kind = step[0]
                if kind == "mask":
                    _, n, kb, i = step
                    s = GH * block_of[n, kb] + i
                    pool.wait_ge(probs_ready, s + 1)
                    diagonal = probs[:, s % PSLOTS, 0:P]
                    nc.gpsimd.affine_select(out=diagonal, in_=diagonal, compare_op=ALU.is_ge, fill=zero, base=0,
                                            pattern=[[1, P]], channel_multiplier=-1).then_inc(probs_masked, 1)
                elif kind == "ln_norm":
                    l = step[1]
                    pool.wait_ge(ln_stats, l + 1)
                    if l >= 2:
                        pool.wait_ge(xn_ready, TB * (l - 1))
                    link(nc.gpsimd.tensor_tensor(norm[:, l % 2, 0], var_mean[:, 0], minus_half[:], ALU.pow))
                    nc.gpsimd.tensor_tensor(norm[:, l % 2, 1], var_mean[:, 1], norm[:, l % 2, 0], ALU.mult)\
                        .then_inc(norm_ready, 1)
                    if l == 0:
                        nc.gpsimd.memset(values[:], 1.0).then_inc(ones_ready, 1)
                        pool.wait_ge(ones_ready, 3)
                    for slot in ([l] if l < NT - 1 else [l, l + 1] if l == NT - 1 else []):
                        pool.wait_ge(norm_ready, l + 1)
                        nc.gpsimd.memset(keys[KR:KM, slot].rearrange("p h t -> p (h t)").bitcast(U32), 0x3F803F80)\
                            .then_inc(key_ones, 1)
                        pool.wait_ge(key_ones, slot + 1)
                elif kind == "split" and step[1][1] > 0:
                    split_product(pool, nc.gpsimd, link, number[step[1]])
                elif kind == "max_parts":
                    n = step[1]
                    pool.wait_ge(neg_max_ready, n + 1)
                    if n >= 2:
                        pool.wait_ge(work_ready, unit_of["turn_max", n - 2] + 1)
                    m, mp = neg_max[:, n % 2], max_parts[:, n % 2]
                    link(nc.gpsimd.tensor_scalar(mp[:, 0], m, 1.0, 1.0, ALU.mult, ALU.mult))
                    link(nc.gpsimd.tensor_tensor(max_rest[:], m, mp[:, 0], ALU.subtract))
                    link(nc.gpsimd.tensor_scalar(mp[:, 1], max_rest[:], 1.0, 1.0, ALU.mult, ALU.mult))
                    nc.gpsimd.tensor_tensor(mp[:, 2], max_rest[:], mp[:, 1], ALU.subtract)\
                        .then_inc(max_parts_ready, 1)
                elif kind == "attn_norm":
                    _, j, c = step
                    pool.wait_ge(ctx_loaded[c], 32 * (j + 1))
                    nc.gpsimd.tensor_tensor(ctx_in[:, c], ctx_in[:, c], recip_in[:, c], ALU.mult)\
                        .then_inc(ctx_normed, 1)
                elif kind == "mix_old":
                    j = step[1]
                    pool.wait_ge(xT_ready, NC * (NT + j + 1))
                    if j == 0:
                        pool.wait_ge(one_minus_ready, 1)
                        pool.wait_ge(ones_ready, 2)
                        pool.wait_ge(work_ready, last_prologue_unit[NT - 1] + 1)
                    else:
                        pool.wait_ge(work_ready, unit_of["gate", j - 1, 1] + 1)
                    for a, m in enumerate((mixk, mixr)):
                        for c in range(NC):
                            nc.gpsimd.tensor_scalar(m[:, c], x2T[:, c, 0:T], one_minus_mu[:, a, c:c + 1], 1.0,
                                                    ALU.mult, ALU.mult).then_inc(mix_prev, 1)
                elif kind == "square":
                    oc = step[1][2]
                    pool.wait_ge(relu_ready, number[step] + 1)
                    nc.gpsimd.tensor_tensor(hidden[:, oc], hidden[:, oc], hidden[:, oc], ALU.mult)\
                        .then_inc(hidden_ready, 1)
                elif kind == "halve":
                    i2 = step[1][2]
                    pool.wait_ge(tanh_ready, number[step] + 1)
                    nc.gpsimd.tensor_scalar(gate[:, i2], gate[:, i2], 0.5, 0.5, ALU.mult, ALU.add)\
                        .then_inc(gate_ready, 1)
                elif kind == "output":
                    i2 = step[1][2]
                    pool.wait_ge(y_ready, number[step] + 1)
                    xo = x2[:, 2 * i2:2 * i2 + 2].rearrange("p a c -> p (a c)")
                    nc.gpsimd.tensor_tensor(xo, xo, gate[:, i2], ALU.add).then_inc(out_ready, 1)

        @block.scalar
        def _(act):
            for step in plan:
                kind = step[0]
                u = unit_of.get(step)
                if kind == "score":
                    _, n, kb, i = step
                    s = GH * block_of[n, kb] + i
                    cols = T - P * max(0, kb - TB * tile_of(n))
                    act.wait_ge(scores_ready, s + 1)
                    if s >= PSLOTS:
                        act.wait_ge(values_done, (s - PSLOTS) // GH + 1)
                    nc.scalar.activation(probs[:, s % PSLOTS, 0:cols], scores[:, s % SRING, 0:cols], ACT.Exp)\
                        .then_inc(probs_ready, 1)
                elif kind == "ctx_out":
                    n = step[1]
                    act.wait_ge(values_done, last_block[n] + 1)
                    if n >= 2:
                        act.wait_ge(ctx_stored[n % 2], 16 * (n // 2))
                    nc.scalar.copy(ctx_sb[:, n % 2], ctx_ps[:, n % CBANKS]).then_inc(ctx_ready, 1)
                elif kind == "normalize":
                    l = step[1]
                    act.wait_ge(norm_ready, l + 1)
                    if l:
                        act.wait_ge(work_ready, unit_of["turn", l - 1, NC - 1] + 1)
                    src = x_in[:, l % 2] if l < NT else x2
                    for i in range(TB):
                        nc.scalar.activation(xn[:, i], src[:, i], ACT.Identity, bias=norm[:, l % 2, 1, i:i + 1],
                                             scale=norm[:, l % 2, 0, i:i + 1]).then_inc(xn_ready, 1)
                elif kind == "turn":
                    _, l, c = step
                    if l < NT:
                        if l:
                            act.wait_ge(work_ready, last_prologue_unit[l - 1] + 1)
                        dst = xnT[:, c]
                    else:
                        if l > NT:
                            act.wait_ge(mix_ready, 4 * (l - NT))
                            act.wait_ge(xT_ready, NC * l)
                            nc.scalar.copy(x2T[:, c, 0:1], x2T[:, c, T:T + 1]).then_inc(last_token_kept, 1)
                            act.wait_ge(last_token_kept, NC * (l - NT - 1) + c + 1)
                        dst = x2T[:, c, 1:T + 1]
                    act.wait_ge(work_ready, u + 1)
                    nc.scalar.copy(dst, work[:, u % RING]).then_inc(xT_ready, 1)
                elif kind in ("key", "query"):
                    i = number[step]
                    act.wait_ge(work_ready, u + 1)
                    if i >= 2:
                        act.wait_ge(parts_ready, i - 1)
                    nc.scalar.mul(rest[:, i % 2], work[:, u % RING], 1.0 if kind == "key" else DK ** -0.5)\
                        .then_inc(product_kept, 1)
                elif kind == "value":
                    _, j, i2 = step
                    act.wait_ge(work_ready, u + 1)
                    act.wait_ge(ones_ready, 3)
                    if j:
                        act.wait_ge(v_stored, 16 * j)
                    src = work[:, u % RING].rearrange("p (a f h d) -> p a f h d", a=2, f=2, d=DK)
                    for f, dst in enumerate((values[:, j], v_out)):
                        d4 = dst[:, 2 * VB * i2:2 * VB * (i2 + 1)].rearrange("p (a h v) -> p a h v", a=2, v=VW)
                        for a in range(2):
                            last = nc.scalar.copy(d4[:, a, :, 0:DK], src[:, a, f])
                    last.then_inc(v_ready, 1)
                elif kind == "turn_max":
                    n = step[1]
                    act.wait_ge(work_ready, u + 1)
                    if n >= 2:
                        act.wait_ge(m_loaded[(n - 2) % QSLOTS], 48 * ((n - 2) // QSLOTS + 1))
                    nc.scalar.copy(max_turned[:, n % 2], work[0:3 * GH * TB, u % RING].bitcast(BF16)[:, 0:P])\
                        .then_inc(max_turned_ready, 1)
                elif kind == "up":
                    _, j, oc = step
                    act.wait_ge(work_ready, u + 1)
                    if j:
                        act.wait_ge(work_ready, unit_of["down", j - 1, 1] + 1)
                    nc.scalar.activation(hidden[:, oc], work[:, u % RING], ACT.Relu).then_inc(relu_ready, 1)
                elif kind == "gate":
                    _, j, i2 = step
                    act.wait_ge(work_ready, u + 1)
                    if j:
                        act.wait_ge(out_ready, 2 * j)
                    nc.scalar.activation(gate[:, i2], work[:, u % RING], ACT.Tanh, scale=0.5)\
                        .then_inc(tanh_ready, 1)

        @block.vector
        def _(dve):
            chain = [0]

            def link(ins):
                chain[0] += 1
                ins.then_inc(dve_chain, 1)
                dve.wait_ge(dve_chain, chain[0])

            first_ln2 = True
            for step in plan:
                kind = step[0]
                u = unit_of.get(step)
                if kind == "max":
                    _, n, i, qt, p = step
                    cols = T if p < tile_of(n) else P * (qt + 1)
                    dve.wait_ge(work_ready, u + 1)
                    bank, row = work[:, u % RING, 0:cols], row_max[:, n % 2, TB * i + qt, p:p + 1]
                    if p < tile_of(n):
                        nc.vector.reduce_max(row, bank, AXX).then_inc(max_done, 1)
                    else:
                        if n == 0:
                            dve.wait_ge(mask_made, 1)
                        nc.vector.tensor_tensor_reduce(bank, bank, mask[:, T - cols:T], 1.0, LOWEST,
                                                       ALU.add, ALU.max, row).then_inc(max_done, 1)
                elif kind == "negmax":
                    n = step[1]
                    dve.wait_ge(max_done, max_through[n])
                    if n >= 2:
                        dve.wait_ge(max_parts_ready, n - 1)
                    nc.vector.tensor_reduce(neg_max[:, n % 2], row_max[:, n % 2, :, 0:tile_of(n) + 1], AXX, ALU.max,
                                            negate=True).then_inc(neg_max_ready, 1)
                elif kind == "ln":
                    l = step[1]
                    if l < NT:
                        dve.wait_ge(x_loaded[l % 2], 16 * (l // 2 + 1))
                    else:
                        dve.wait_ge(x2_ready, 2 * (l - NT) + 1)
                    if l:
                        dve.wait_ge(norm_ready, l)
                    src = x_in[:, l % 2] if l < NT else x2
                    for i in range(TB):
                        if l >= NT and i == TB // 2:
                            dve.wait_ge(x2_ready, 2 * (l - NT + 1))
                        last = nc.vector.bn_stats(bn[:, i], src[:, i])
                    link(last)
                    for i in range(TB):
                        last = nc.vector.bn_aggr(mean_var[:, i], bn[:, i])
                    link(last)
                    nc.vector.tensor_scalar(var_mean[:, 0], mean_var[:, :, 1], EPS, None, ALU.add)
                    nc.vector.tensor_scalar(var_mean[:, 1], mean_var[:, :, 0], -1.0, None, ALU.mult)\
                        .then_inc(ln_stats, 1)
                elif kind == "split" and step[1][1] == 0:
                    split_product(dve, nc.vector, link, number[step[1]])
                elif kind == "sums":
                    dve.wait_ge(sums_loaded, 16 * (number[step] + 1))
                    nc.vector.reciprocal(sums[:], sums[:]).then_inc(sums_ready, 1)
                elif kind == "residual":
                    _, j, i2 = step[1]
                    u = unit_of[step[1]]
                    dve.wait_ge(work_ready, u + 1)
                    dve.wait_ge(x_loaded[j % 2], 16 * ((NT + j) // 2 + 1))
                    if j:
                        dve.wait_ge(out_stored, 16 * j)
                    nc.vector.tensor_tensor(x2[:, 2 * i2:2 * i2 + 2],
                                            work[:, u % RING].rearrange("p (a c) -> p a c", a=2),
                                            x_in[:, j % 2, 2 * i2:2 * i2 + 2], ALU.add).then_inc(x2_ready, 1)
                elif kind == "mix":
                    j = step[1]
                    if first_ln2:
                        first_ln2 = False
                        dve.wait_ge(mu_loaded, 32)
                        nc.vector.tensor_scalar(one_minus_mu[:], mu[:], -1.0, 1.0, ALU.mult, ALU.add)\
                            .then_inc(one_minus_ready, 1)
                    for a, m in enumerate((mixk, mixr)):
                        for c in range(NC):
                            dve.wait_ge(mix_prev, 4 * j + 2 * a + c + 1)
                            nc.vector.scalar_tensor_tensor(out=m[:, c], in0=x2T[:, c, 1:T + 1],
                                                           scalar=mu[:, a, c:c + 1], in1=m[:, c],
                                                           op0=ALU.mult, op1=ALU.add).then_inc(mix_ready, 1)
                elif kind == "gated":
                    i2 = step[1][2]
                    u = unit_of[step[1]]
                    dve.wait_ge(work_ready, u + 1)
                    dve.wait_ge(gate_ready, number[step] + 1)
                    nc.vector.tensor_tensor(gate[:, i2], work[:, u % RING], gate[:, i2], ALU.mult)\
                        .then_inc(y_ready, 1)

        @block.tensor
        def _(pe):
            def own_bank(u):
                if u >= RING:
                    before = units[u - RING]
                    pe.wait_ge(released_by[before[0]], number[before] + 1)
                return work[:, u % RING]

            pe.wait_ge(consts_ready, 2)
            for step in plan:
                kind = step[0]
                u = unit_of.get(step)
                if kind == "score":
                    _, n, kb, i = step
                    j, half = tile_of(n), half_of(n)
                    off = P * max(0, kb - TB * j)
                    slot = kslot(half, kb // TB)
                    s = GH * block_of[n, kb] + i
                    if kb == 0 and i == 0:
                        pe.wait_ge(m_loaded[n % QSLOTS], 48 * (n // QSLOTS + 1))
                    if kb % TB == 0 and i == 0:
                        pe.wait_ge(key_ones, slot + 1)
                        pe.wait_ge(k_loaded[slot], 16 * slot_loads(half, kb // TB))
                    if s >= SRING:
                        pe.wait_ge(probs_ready, s - SRING + 1)
                    last = nc.tensor.matmul(scores[:, s % SRING, 0:T - off],
                                            keys[0:KM, slot, GH * (n % 2) + i, P * (kb % TB):P * (kb % TB + 1)],
                                            queries[0:KM, n % QSLOTS, i, off:T], start=True, stop=True)
                    last.then_inc(scores_ready, 1)
                elif kind == "probs_values":
                    _, n, kb = step
                    off = P * max(0, kb - TB * tile_of(n))
                    g = block_of[n, kb]
                    half, c = half_of(n), kb // TB
                    pe.wait_ge(probs_ready, GH * (g + 1))
                    if kb >= TB * tile_of(n):
                        pe.wait_ge(probs_masked, number["mask", n, kb, GH - 1] + 1)
                    if kb == 0 and n >= CBANKS:
                        pe.wait_ge(ctx_ready, n - CBANKS + 1)
                    if half == 0 and kb % TB == 0:
                        pe.wait_ge(v_ready, 2 * (c + 1))
                    elif half == 1 and kb % TB == 0:
                        pe.wait_ge(v_loaded[kslot(1, c)], 16)
                    for i in range(GH):
                        v0 = VB * (kb % TB) + VW * (GH * (n % 2) + i)
                        last = nc.tensor.matmul(ctx_ps[32 * i:32 * i + 32, n % CBANKS, off:T],
                                                values[:, kslot(half, c), v0:v0 + 32],
                                                probs[:, (GH * g + i) % PSLOTS, 0:T - off],
                                                start=(kb == 0), stop=(kb == TB * (tile_of(n) + 1) - 1),
                                                tile_position=(0, 32 * i))
                    last.then_inc(values_done, 1)
                elif kind == "max":
                    _, n, i, qt, p = step
                    half = half_of(n)
                    cols = T if p < tile_of(n) else P * (qt + 1)
                    if i == 0 and qt == 0:
                        if p == 0:
                            pe.wait_ge(q_loaded[n % QSLOTS], 16 * (n // QSLOTS + 1))
                        pe.wait_ge(k_loaded[kslot(half, p)], 16 * slot_loads(half, p))
                    bank = own_bank(u)
                    last = nc.tensor.matmul(bank[:, 0:cols], queries[0:KR, n % QSLOTS, i, P * qt:P * (qt + 1)],
                                            keys[0:KR, kslot(half, p), GH * (n % 2) + i, 0:cols],
                                            start=True, stop=True)
                    last.then_inc(work_ready, 1)
                elif kind == "turn_max":
                    n = step[1]
                    pe.wait_ge(max_parts_ready, n + 1)
                    bank = own_bank(u)
                    nc.tensor.transpose(bank[0:3 * GH * TB].bitcast(BF16)[:, 0:P],
                                        max_parts[:, n % 2].rearrange("p r m -> p (r m)"), ident_b[:])\
                        .then_inc(work_ready, 1)
                elif kind == "turn":
                    _, l, c = step
                    bank = own_bank(u)
                    for i in range(TB):
                        if c == 0:
                            pe.wait_ge(xn_ready, TB * l + i + 1)
                        last = nc.tensor.transpose(bank[:, P * i:P * (i + 1)], xn[:, i, P * c:P * (c + 1)], ident[:])
                    last.then_inc(work_ready, 1)
                elif kind in ("key", "query", "up"):
                    _, j, oc = step
                    if kind == "up":
                        pe.wait_ge(mix_ready, 4 * j + 2)
                    else:
                        pe.wait_ge(xT_ready, NC * (j + 1))
                    name = {"key": "wk", "query": "wq", "up": "wkf"}[kind]
                    if j == 0:
                        pe.wait_ge(w_loaded[name], 16)
                    rhs = mixk if kind == "up" else xnT
                    bank = own_bank(u)
                    for c in range(NC):
                        last = nc.tensor.matmul(bank, w[name][:, c, P * oc:P * (oc + 1)], rhs[:, c],
                                                start=(c == 0), stop=(c == NC - 1))
                    last.then_inc(work_ready, 1)
                elif kind in ("value", "attn_out", "gate", "down"):
                    _, j, i2 = step
                    if kind == "value":
                        pe.wait_ge(xT_ready, NC * (j + 1))
                    elif kind == "attn_out":
                        pe.wait_ge(ctx_normed, NC * (j + 1))
                    elif kind == "gate":
                        pe.wait_ge(mix_ready, 4 * (j + 1))
                    else:
                        pe.wait_ge(hidden_ready, 2 * (j + 1))
                    name, lhs = {"value": ("wv", xnT), "attn_out": ("wo", ctx_in), "gate": ("wr", mixr),
                                 "down": ("wvf", hidden)}[kind]
                    if j == 0:
                        pe.wait_ge(w_loaded[name], 16)
                    bank = own_bank(u)
                    for a in range(2):
                        t0 = P * (2 * i2 + a)
                        for c in range(NC):
                            last = nc.tensor.matmul(bank[:, D * a:D * (a + 1)], lhs[:, c, t0:t0 + P], w[name][:, c],
                                                    start=(c == 0), stop=(c == NC - 1))
                    last.then_inc(work_ready, 1)


def kernel(L0_attn_x, L0_attn_wq, L0_attn_wk, L0_attn_wv, L0_attn_wo, L0_ffn_W_r, L0_ffn_W_k, L0_ffn_W_v,
           L0_ffn_mu_r, L0_ffn_mu_k):
    import numpy as np
    import concourse.bacc as bacc
    from concourse.bass_utils import run_bass_kernel_spmd

    x = np.asarray(L0_attn_x)
    laid_out = {"x": x.reshape(x.shape[1], x.shape[2])}
    for name, weight in (("wq_t", L0_attn_wq), ("wk_t", L0_attn_wk), ("wv_t", L0_attn_wv), ("wo_t", L0_attn_wo),
                         ("wr_t", L0_ffn_W_r), ("wkf_t", L0_ffn_W_k), ("wvf_t", L0_ffn_W_v)):
        w_t = np.asarray(weight).T
        if name in ("wq_t", "wk_t"):
            w_t = w_t.reshape(D, 2, HALF, DK).transpose(0, 1, 3, 2).reshape(D, D)
        laid_out[name] = np.ascontiguousarray(w_t)
    for name, mix in (("mu_r", L0_ffn_mu_r), ("mu_k", L0_ffn_mu_k)):
        laid_out[name] = np.ascontiguousarray(np.asarray(mix).reshape(NC, P).T)
    nc = bacc.Bacc("TRN2", target_bir_lowering=False, num_devices=1)
    args = {name: nc.dram_tensor(name, a.shape, mybir.dt.from_np(a.dtype), kind="ExternalInput").ap()
            for name, a in laid_out.items()}
    out = nc.dram_tensor("out", (S, D), F32, kind="ExternalOutput").ap()
    attention_ffn(nc, out=out, **args)
    result = run_bass_kernel_spmd(nc, [laid_out], core_ids=[0])
    return result.results[0]["out"].reshape(x.shape)
```
